# Optimizing a Trainium2 kernel written in Bass

```python
import numpy as np
import jax
import jax.numpy as jnp

def _softmax(x, axis=-1):
    return jax.nn.softmax(x, axis=axis)

def _gelu(x):
    return jax.nn.gelu(x, approximate=True)

def _silu(x):
    return jax.nn.silu(x)

def _sigmoid(x):
    return jax.nn.sigmoid(x)

def _layernorm(x, axis=-1, eps=1e-05):
    m = jnp.mean(x, axis=axis, keepdims=True)
    v = jnp.var(x, axis=axis, keepdims=True)
    return (x - m) / jnp.sqrt(v + eps)

def _scatter_add(tgt, idx, src, axis=0):
    return tgt.at[idx].add(src)

def _segment_sum(src, seg, n):
    return jax.ops.segment_sum(src, seg, n)
kernel_name = 'mk_adaln_d1_jaxref_r8_bdf319'

def setup_inputs(seed: int=0):
    np.random.seed(seed)
    _w = jnp.asarray

    def _L0_attn_setup():
        import jax, jax.numpy as jnp
        import numpy as np
        from jax import lax

        def _silu(x):
            return x * jax.nn.sigmoid(x)

        def _selective_scan(u, delta, A, B, C):
            b, l, d = u.shape
            n = A.shape[1]
            deltaA = jnp.exp(delta[..., None] * A)
            deltaBu = (delta * u)[..., None] * B[:, :, None, :]

            def step(h, inp):
                dA, dBu, c = inp
                h = dA * h + dBu
                y = jnp.einsum('bdn,bn->bd', h, c)
                return (h, y)
            h0 = jnp.zeros((b, d, n), u.dtype)
            xs = (jnp.moveaxis(deltaA, 1, 0), jnp.moveaxis(deltaBu, 1, 0), jnp.moveaxis(C, 1, 0))
            _, ys = lax.scan(step, h0, xs)
            return jnp.moveaxis(ys, 0, 1)
        key = jax.random.key(seed)
        ks = jax.random.split(key, 9)
        b, l, h = (2, 256, 128)
        d, n, r, k = (256, 16, 64, 4)
        s = lambda *sh: 1.0 / np.sqrt(sh[-1])
        return {'x': jax.random.normal(ks[0], (b, l, h), jnp.float32), 'W_in': jax.random.normal(ks[1], (2 * d, h), jnp.float32) * s(h), 'conv_w': jax.random.normal(ks[2], (d, 1, k), jnp.float32) * s(k), 'conv_b': jax.random.normal(ks[3], (d,), jnp.float32) * 0.02, 'W_x': jax.random.normal(ks[4], (r + 2 * n, d), jnp.float32) * s(d), 'W_dt': jax.random.normal(ks[5], (d, r), jnp.float32) * s(r), 'b_dt': jax.random.normal(ks[6], (d,), jnp.float32) * 0.02, 'A_log': jax.random.normal(ks[7], (d, n), jnp.float32) * 0.1, 'W_out': jax.random.normal(ks[8], (h, d), jnp.float32) * s(d)}
    _L0_attn_in = _L0_attn_setup()

    def _L0_ffn_setup():
        import jax, jax.numpy as jnp
        import numpy as np
        NUM_EXPERTS = 8
        HIDDEN = 128
        FFN = 512
        BATCH = 2
        SEQ = 256
        key = jax.random.key(seed)
        k_x, k_g, k_u, k_d = jax.random.split(key, 4)
        scale_in = 1.0 / np.sqrt(HIDDEN)
        scale_mid = 1.0 / np.sqrt(FFN)
        return {'hidden_states': jax.random.normal(k_x, (BATCH, SEQ, HIDDEN), dtype=jnp.float32), 'Wg': jax.random.normal(k_g, (NUM_EXPERTS, HIDDEN, FFN), dtype=jnp.float32) * scale_in, 'Wu': jax.random.normal(k_u, (NUM_EXPERTS, HIDDEN, FFN), dtype=jnp.float32) * scale_in, 'Wd': jax.random.normal(k_d, (NUM_EXPERTS, FFN, HIDDEN), dtype=jnp.float32) * scale_mid}
    _L0_ffn_in = _L0_ffn_setup()
    _L0_c = _w((lambda *s: np.random.randn(*s).astype(np.float32) * 0.05)(2, 128))
    _L0_wmod = _w((lambda *s: np.random.randn(*s).astype(np.float32) * 0.05)(128, 6 * 128) * 128 ** (-0.5))
    _d = {'L0_attn_x': _L0_attn_in['x'], 'L0_attn_W_in': _L0_attn_in['W_in'], 'L0_attn_conv_w': _L0_attn_in['conv_w'], 'L0_attn_conv_b': _L0_attn_in['conv_b'], 'L0_attn_W_x': _L0_attn_in['W_x'], 'L0_attn_W_dt': _L0_attn_in['W_dt'], 'L0_attn_b_dt': _L0_attn_in['b_dt'], 'L0_attn_A_log': _L0_attn_in['A_log'], 'L0_attn_W_out': _L0_attn_in['W_out'], 'L0_ffn_Wg': _L0_ffn_in['Wg'], 'L0_ffn_Wu': _L0_ffn_in['Wu'], 'L0_ffn_Wd': _L0_ffn_in['Wd'], 'L0_c': _L0_c, 'L0_wmod': _L0_wmod}
    _x0 = _d['L0_attn_x']
    _d['L0_attn_x'] = jax.random.normal(jax.random.fold_in(jax.random.key(seed), 1), (2, 2048, 128), dtype=_x0.dtype)
    del _x0
    return _d

def reference(L0_attn_x, L0_attn_W_in, L0_attn_conv_w, L0_attn_conv_b, L0_attn_W_x, L0_attn_W_dt, L0_attn_b_dt, L0_attn_A_log, L0_attn_W_out, L0_ffn_Wg, L0_ffn_Wu, L0_ffn_Wd, L0_c, L0_wmod):

    def _L0_attn_ref(x, W_in, conv_w, conv_b, W_x, W_dt, b_dt, A_log, W_out):
        import jax, jax.numpy as jnp
        import numpy as np
        from jax import lax

        def _silu(x):
            return x * jax.nn.sigmoid(x)

        def _selective_scan(u, delta, A, B, C):
            b, l, d = u.shape
            n = A.shape[1]
            deltaA = jnp.exp(delta[..., None] * A)
            deltaBu = (delta * u)[..., None] * B[:, :, None, :]

            def step(h, inp):
                dA, dBu, c = inp
                h = dA * h + dBu
                y = jnp.einsum('bdn,bn->bd', h, c)
                return (h, y)
            h0 = jnp.zeros((b, d, n), u.dtype)
            xs = (jnp.moveaxis(deltaA, 1, 0), jnp.moveaxis(deltaBu, 1, 0), jnp.moveaxis(C, 1, 0))
            _, ys = lax.scan(step, h0, xs)
            return jnp.moveaxis(ys, 0, 1)
        b, l, _ = x.shape
        d, n = A_log.shape
        r = W_dt.shape[1]
        k = conv_w.shape[-1]
        xr = jnp.einsum('blh,eh->ble', x, W_in)
        xs, res = (xr[..., :d], xr[..., d:])
        xp = jnp.pad(xs, ((0, 0), (k - 1, 0), (0, 0)))
        xc = lax.conv_general_dilated(jnp.transpose(xp, (0, 2, 1)), conv_w, (1,), 'VALID', dimension_numbers=('NCH', 'OIH', 'NCH'), feature_group_count=d)
        xc = jnp.transpose(xc, (0, 2, 1)) + conv_b
        xc = _silu(xc)
        x_dbl = jnp.einsum('bld,ed->ble', xc, W_x)
        dt, B, C = (x_dbl[..., :r], x_dbl[..., r:r + n], x_dbl[..., r + n:])
        delta = jax.nn.softplus(jnp.einsum('blr,dr->bld', dt, W_dt) + b_dt)
        A = -jnp.exp(A_log.astype(jnp.float32))
        y = lax.stop_gradient(_selective_scan(xc, delta, A, B, C))
        return jnp.einsum('bld,hd->blh', y * _silu(res), W_out)

    def _L0_ffn_ref(hidden_states, Wg, Wu, Wd):
        import jax, jax.numpy as jnp
        import numpy as np
        NUM_EXPERTS = 8
        HIDDEN = 128
        FFN = 512
        BATCH = 2
        SEQ = 256
        B, S, H = hidden_states.shape
        x = hidden_states.reshape(-1, H)

        def expert_step(acc, w):
            wg, wu, wd = w
            h = jax.nn.silu(x @ wg) * (x @ wu)
            return (acc + h @ wd, None)
        acc, _ = jax.lax.scan(expert_step, jnp.zeros_like(x), (Wg, Wu, Wd))
        return acc.reshape(B, S, H)
    x = L0_attn_x
    mod = (_silu(L0_c) @ L0_wmod).reshape(L0_c.shape[0], 6, 1, -1)
    sa, ca, ga, sb, cb, gb = (mod[:, 0], mod[:, 1], mod[:, 2], mod[:, 3], mod[:, 4], mod[:, 5])
    ga = (2 * (ga >= 0) - 1) * jnp.maximum(jnp.abs(ga), 0.25)
    gb = (2 * (gb >= 0) - 1) * jnp.maximum(jnp.abs(gb), 0.25)
    h = _layernorm(x, axis=-1) * (1 + ca) + sa
    x = x + ga * _L0_attn_ref(h, L0_attn_W_in, L0_attn_conv_w, L0_attn_conv_b, L0_attn_W_x, L0_attn_W_dt, L0_attn_b_dt, L0_attn_A_log, L0_attn_W_out)
    h = _layernorm(x, axis=-1) * (1 + cb) + sb
    x = x + gb * _L0_ffn_ref(h, L0_ffn_Wg, L0_ffn_Wu, L0_ffn_Wd)
    return x

_drawn_inputs = setup_inputs


def setup_inputs(seed=0):
    import zlib

    import numpy as np

    out = dict(_drawn_inputs(seed))
    spreads = {}
    factors = {'L0_attn_conv_b': 8.0, 'L0_attn_b_dt': 8.0, 'L0_attn_A_log': 5.579}
    for name, (base, spread) in spreads.items():
        noise = np.random.default_rng([zlib.crc32(name.encode()), seed]).standard_normal(out[name].shape)
        drawn = base * np.exp(spread * noise) if base else spread * noise
        out[name] = jnp.asarray(drawn.astype(out[name].dtype))
    for name, factor in factors.items():
        out[name] = (out[name] * factor).astype(out[name].dtype)
    return out
```

```python
from contextlib import ExitStack

import concourse.bass as bass
from concourse import mybir

F32 = mybir.dt.float32
F32R = mybir.dt.float32r
ALU = mybir.AluOpType
ACT = mybir.ActivationFunctionType

P = 128
B, S, H = 2, 2048, 128
D, N, R, K = 256, 16, 64, 4
NE, F = 8, 512
L = 512
NC = B * S // L
CB = S // L
HALVES = D // P
PAIRS = N // 2
UNITS = PAIRS * HALVES
TB = L // P
FB = F // P
NB = NE * FB
PARTS = 4
BLOCKS = NB // PARTS
SLOTS = 8
EPS = 1e-5
MISC_PRE, MISC_POST = 6, 4
MISC = MISC_PRE + MISC_POST


def is_first(c):
    return isinstance(c, int) and c == 0


def build(nc, x, w_in, cols_in, w_x, w_dt, a_log, w_out, w_gu, w_d, c_t, w_mod, out, bc_dram):
    with ExitStack() as ctx:
        def sb(name, shape, dt=F32):
            return ctx.enter_context(nc.sbuf_tensor(name, shape, dt))

        def bank(name):
            return ctx.enter_context(nc.psum_tensor(name, [P, 512], F32))

        def sem(name):
            return ctx.enter_context(nc.semaphore(name))

        gu_hi = sb("gu_hi", [P, NE, 2, F], F32R)
        gu_lo = sb("gu_lo", [P, NE, 2, F], F32R)
        wd = sb("wd", [P, NB, H])
        w_in_sb = sb("w_in_sb", [P, 2 * D])
        w_x_sb = sb("w_x_sb", [P, HALVES, R + 2 * N])
        w_dt_sb = sb("w_dt_sb", [R, D])
        w_out_sb = sb("w_out_sb", [P, HALVES, H])
        w_out_ga = sb("w_out_ga", [P, B, HALVES, H])
        cols = sb("cols", [P, HALVES, K + 2])
        a_neg = sb("a_neg", [P, HALVES, N])
        ident = sb("ident", [P, P])
        c_sb = sb("c_sb", [P, B])
        sc = sb("sc", [P, B])
        sc_wide = sb("sc_wide", [P, B, P])
        mod_sb = sb("mod_sb", [P, B, 6])
        ga_row = sb("ga_row", [P, B, H])
        ga_sign = sb("ga_sign", [P, B, H])
        gb_sign = sb("gb_sign", [P, B])
        minus_half = sb("minus_half", [P, TB])
        tok = sb("tok", [P, TB, H])
        ln_in = sb("ln_in", [P, 2, TB, 6])
        ln_mv = sb("ln_mv", [P, 2, TB, 2])
        ln_ve = sb("ln_ve", [P, 2, TB])
        ln_rstd = sb("ln_rstd", [P, 2, TB])
        h1 = sb("h1", [P, L])
        xs_ext = sb("xs_ext", [P, K - 1 + L])
        halo = sb("halo", [P, CB + 1, HALVES, K - 1])
        xc = sb("xc", [P, HALVES, L])
        x_dbl = sb("x_dbl", [P, L])
        log_part = sb("log_part", [P, HALVES, L])
        delta = sb("delta", [P, HALVES, L])
        du = sb("du", [P, HALVES, L])
        ring = sb("ring", [P, SLOTS, 2, L])
        b_tile = sb("b_tile", [P, 2, 2, L])
        c_tile = sb("c_tile", [P, 4, 2, L])
        carry = sb("carry", [P, CB + 1, HALVES, N])
        y = sb("y", [P, HALVES, L])
        gate = sb("gate", [P, HALVES, L])
        x1 = sb("x1", [P, 2, TB, H])
        tok2 = sb("tok2", [P, TB, H])
        h2 = sb("h2", [P, L])
        h2_hi = sb("h2_hi", [P, L], F32R)
        h2_lo = sb("h2_lo", [P, L], F32R)
        p_tile = sb("p_tile", [P, BLOCKS, L])
        f_t = h2

        g_bank = [bank("g0"), bank("g1")]
        u_bank = [bank("u0"), bank("u1")]
        acc = bank("acc")
        dbu_bank = [bank("dbu0"), bank("dbu1")]
        misc = bank("misc")

        small_in, gu_in, wd_in = sem("small_in"), sem("gu_in"), sem("wd_in")
        dve_set, act_set, pe_set, pool_set = sem("dve_set"), sem("act_set"), sem("pe_set"), sem("pool_set")
        hi_done, lo_done = sem("hi_done"), sem("lo_done")
        x_loaded, xres_loaded, out_stored, bc_stored = sem("x_loaded"), sem("xres_loaded"), sem("out_stored"), sem("bc_stored")
        b_loaded = [sem(f"b_loaded{i}") for i in range(2)]
        c_loaded = [sem(f"c_loaded{i}") for i in range(4)]
        bc_seen = sem("bc_seen")
        misc_filled, misc_drained = sem("misc_filled"), sem("misc_drained")
        ln_step = [sem("ln1_step"), sem("ln2_step")]
        ln_ready = [sem("ln1_ready"), sem("ln2_ready")]
        xn_ready = [sem("xn1_ready"), sem("xn2_ready")]
        h1_ready, xs_ready, halo_in, conv_step, conv_done, xc_ready = (
            sem("h1_ready"), sem("xs_ready"), sem("halo_in"), sem("conv_step"), sem("conv_done"), sem("xc_ready"))
        xdbl_ready, sp_step, sp_ready, delta_ready, du_ready = (
            sem("xdbl_ready"), sem("sp_step"), sem("sp_ready"), sem("delta_ready"), sem("du_ready"))
        exp_done, dbu_done, scan_step, scan_done, pool_step, unit_reduced = (
            sem("exp_done"), sem("dbu_done"), sem("scan_step"), sem("scan_done"), sem("pool_step"), sem("unit_reduced"))
        gate_ready, r_ready, x1_ready, h2_full, h2_step, h2_ready = (
            sem("gate_ready"), sem("r_ready"), sem("x1_ready"), sem("h2_full"), sem("h2_step"), sem("h2_ready"))
        g_ready, u_ready, silu_done, p_ready, acc_ready, ft_ready, ft_turned, out_ready = (
            sem("g_ready"), sem("u_ready"), sem("silu_done"), sem("p_ready"), sem("acc_ready"), sem("ft_ready"),
            sem("ft_turned"), sem("out_ready"))

        def chunk_rows(t, c):
            return t[bass.ts(c, P), :]

        def misc_pre(i, k):
            return k if isinstance(i, int) and i < 0 else MISC_PRE + MISC * i + 2 + k

        def misc_post(i, k):
            last = 0 if isinstance(i, int) and i == NC - 1 else MISC_PRE
            return MISC_PRE + MISC * i + k + (last if k >= 2 else 0)

        block = ctx.enter_context(nc.Block())

        @block.sync
        def _(sp):
            def load_x(c):
                if not is_first(c):
                    sp.wait_ge(h1_ready, c)
                sp.dma_start(tok[:].rearrange("p t h -> p (t h)"), chunk_rows(x, c)).then_inc(x_loaded, 16)

            def load_residual(c, stored):
                if stored is not None:
                    sp.wait_ge(out_stored, stored)
                sp.dma_start(x1[:, c % 2].rearrange("p t h -> p (t h)"), chunk_rows(x, c)).then_inc(xres_loaded, 16)

            def store_bc(c):
                sp.wait_ge(xdbl_ready, c + 1)
                sp.dma_start(bc_dram[bass.ts(c, 2 * N), :], x_dbl[R:R + 2 * N, :]).then_inc(bc_stored, 16)

            def load_pair(c, j):
                if j == 0:
                    sp.wait_ge(bc_stored, 16 * (c + 1))
                    sp.sem_inc(bc_seen, 1)
                def rows(first):
                    return bc_dram[bass.ds(2 * N * c + first + 2 * j, 2), :].partition_broadcast(P)
                if not (is_first(c) and j < 2):
                    sp.wait_ge(dbu_done, 2 * N * c + 4 * (j - 1))
                sp.dma_start(b_tile[:, j % 2], rows(0)).then_inc(b_loaded[j % 2], 16)
                if not (is_first(c) and j < 4):
                    sp.wait_ge(unit_reduced, UNITS * c + 2 * (j - 3))
                sp.dma_start(c_tile[:, j % 4], rows(N)).then_inc(c_loaded[j % 4], 16)

            def store_out(c):
                sp.wait_ge(out_ready, c + 1)
                sp.dma_start(chunk_rows(out, c), x1[:, c % 2].rearrange("p t h -> p (t h)")).then_inc(out_stored, 16)

            load_x(0)
            for dst, src in ((c_sb, c_t), (w_in_sb, w_in), (cols, cols_in), (w_x_sb, w_x), (w_dt_sb, w_dt),
                             (a_neg, a_log), (w_out_sb, w_out)):
                sp.dma_start(dst[:], src).then_inc(small_in, 16)
            sp.dma_start(b_tile[:].rearrange("p a b l -> p (a b l)")[:, 0:6 * H], w_mod).then_inc(small_in, 16)
            for e in range(NE):
                sp.dma_start(ring[:, e], w_gu[:, e]).then_inc(gu_in, 16)
                sp.wait_ge(gu_in, 16 * (e + 1))
            load_residual(0, None)
            sp.dma_start(wd[:], w_d).then_inc(wd_in, 16)
            store_bc(0)
            sp.wait_ge(pe_set, 2)
            load_pair(0, 0)
            load_pair(0, 1)

            def body(i, pre=True, ffn=True):
                if pre:
                    load_x(i + 1)
                for j in (2, 3, 4, 5):
                    load_pair(i, j)
                if pre:
                    store_bc(i + 1)
                for j in (6, 7):
                    load_pair(i, j)
                if pre:
                    load_pair(i + 1, 0)
                    load_pair(i + 1, 1)
                if ffn:
                    store_out(i - 1)
                if pre:
                    load_residual(i + 1, 16 * i if ffn else None)

            body(0, ffn=False)
            with sp.Fori(1, NC - 1) as i:
                body(i)
            body(NC - 1, pre=False)
            store_out(NC - 1)
            sp.wait_ge(out_stored, 16 * NC)
            sp.wait_ge(bc_stored, 16 * NC)

        @block.tensor
        def _(pe):
            def use_misc(k):
                if not is_first(k):
                    pe.wait_ge(misc_drained, k)

            def turn(dst, src, s_done):
                for t in range(TB):
                    last = nc.tensor.transpose(dst(t), src(t), ident[:])
                last.then_inc(s_done, 1)

            def pre_turn(c, k):
                use_misc(k)
                pe.wait_ge(xn_ready[0], c + 1)
                turn(lambda t: misc[:, t * P:(t + 1) * P], lambda t: tok[:, t, :], misc_filled)

            def in_proj(c, k, block_):
                use_misc(k)
                pe.wait_ge(h1_ready, c + 1)
                nc.tensor.matmul(misc[:], w_in_sb[:, block_ * P:(block_ + 1) * P], h1[:], start=True,
                                 stop=True).then_inc(misc_filled, 1)

            def x_proj(c, k):
                use_misc(k)
                pe.wait_ge(xc_ready, 2 * c + 2)
                for hf in range(HALVES):
                    last = nc.tensor.matmul(misc[0:R + 2 * N, :], w_x_sb[:, hf, :], xc[:, hf, :],
                                            start=(hf == 0), stop=(hf == 1))
                last.then_inc(misc_filled, 1)

            def dt_proj(c, k, hf):
                use_misc(k)
                pe.wait_ge(xdbl_ready, c + 1)
                nc.tensor.matmul(misc[:], w_dt_sb[:, hf * P:(hf + 1) * P], x_dbl[0:R, :], start=True,
                                 stop=True).then_inc(misc_filled, 1)

            def out_proj(c, k):
                use_misc(k)
                pe.wait_ge(r_ready, 2 * c + 2)
                for t in range(TB):
                    for hf in range(HALVES):
                        r_t = gate[:, hf, :].rearrange("p (q t) -> p t q", t=TB)[:, t, :]
                        last = nc.tensor.matmul(misc[:, t * P:(t + 1) * P], r_t, w_out_ga[:, c // CB, hf, :],
                                                start=(hf == 0), stop=(hf == 1))
                last.then_inc(misc_filled, 1)

            def post_turn(c, k):
                use_misc(k)
                pe.wait_ge(xn_ready[1], c + 1)
                turn(lambda t: misc[:, t * P:(t + 1) * P], lambda t: tok2[:, t, :], misc_filled)

            def gate_up(c, b):
                e, f = b // FB, (b % FB) * P
                if b == 0:
                    pe.wait_ge(h2_ready, c + 1)
                for which, to, used, s_done in ((0, g_bank, silu_done, g_ready), (1, u_bank, p_ready, u_ready)):
                    if b % BLOCKS >= 2:
                        pe.wait_ge(used, NB * c + b - 1)
                    w_hi, w_lo = gu_hi[:, e, which, f:f + P], gu_lo[:, e, which, f:f + P]
                    nc.tensor.matmul(to[b % 2][:], w_hi, h2_hi[:], start=True, stop=False)
                    nc.tensor.matmul(to[b % 2][:], w_hi, h2_lo[:], start=False, stop=False)
                    nc.tensor.matmul(to[b % 2][:], w_lo, h2_hi[:], start=False, stop=True).then_inc(s_done, 1)

            def down(c, b):
                pe.wait_ge(p_ready, NB * c + b + 1)
                last = nc.tensor.matmul(acc[:], wd[:, b, :], p_tile[:, b % BLOCKS, :], start=(b == 0),
                                        stop=(b == NB - 1))
                if b == NB - 1:
                    last.then_inc(acc_ready, 1)

            def ffn_tail(c):
                pe.wait_ge(ft_ready, c + 1)
                turn(lambda t: acc[:, t * P:(t + 1) * P],
                     lambda t: f_t[:].rearrange("p (q t) -> p t q", t=TB)[:, t, :], ft_turned)

            pe.wait_ge(small_in, 16 * 8)
            pe.wait_ge(act_set, 1)
            w_mod_sb = b_tile[:].rearrange("p a b l -> p (a b l)")[:, 0:6 * H]
            for k in range(6):
                last = nc.tensor.matmul(acc[:, B * k:B * k + B], w_mod_sb[:, k * H:(k + 1) * H], sc[:], start=True,
                                        stop=True)
            last.then_inc(pe_set, 1)
            pe.wait_ge(dve_set, 4)
            for b in range(B):
                last = nc.tensor.matmul(u_bank[0][:, b * H:(b + 1) * H], sc_wide[:, b, :],
                                        w_mod_sb[:, 2 * H:3 * H], start=True, stop=True)
            last.then_inc(pe_set, 1)
            pe.wait_ge(pool_set, 2)
            pre_turn(0, 0)
            in_proj(0, 1, 0)
            in_proj(0, 2, 1)
            x_proj(0, 3)
            dt_proj(0, 4, 0)
            dt_proj(0, 5, 1)

            def body(i, pre=True, ffn=True):
                tasks = {}
                tasks[0, 1] = lambda: in_proj(i, misc_post(i, 0), 2)
                tasks[0, 3] = lambda: in_proj(i, misc_post(i, 1), 3)
                if pre:
                    tasks[0, 9] = lambda: pre_turn(i + 1, misc_pre(i, 0))
                    tasks[0, 11] = lambda: in_proj(i + 1, misc_pre(i, 1), 0)
                    tasks[0, 14] = lambda: in_proj(i + 1, misc_pre(i, 2), 1)
                    tasks[1, 6] = lambda: x_proj(i + 1, misc_pre(i, 3))
                    tasks[1, 15] = lambda: dt_proj(i + 1, misc_pre(i, 4), 0)
                    tasks[2, 0] = lambda: dt_proj(i + 1, misc_pre(i, 5), 1)
                tasks[3, 9] = lambda: out_proj(i, misc_post(i, 2))
                tasks[3, 15] = lambda: post_turn(i, misc_post(i, 3))
                for part in range(PARTS):
                    for k in range(2 * BLOCKS):
                        if ffn:
                            (gate_up if k < BLOCKS else down)(i - 1, part * BLOCKS + k % BLOCKS)
                        if (part, k) in tasks:
                            tasks[part, k]()
                if ffn:
                    ffn_tail(i - 1)

            body(0, ffn=False)
            pe.wait_ge(lo_done, NE)
            pe.wait_ge(wd_in, 16)
            with pe.Fori(1, NC - 1) as i:
                body(i)
            body(NC - 1, pre=False)
            for part in range(PARTS):
                for k in range(2 * BLOCKS):
                    (gate_up if k < BLOCKS else down)(NC - 1, part * BLOCKS + k % BLOCKS)
            ffn_tail(NC - 1)

        @block.scalar
        def _(act):
            def turned(c, k, which, dst, s_done):
                act.wait_ge(misc_filled, k + 1)
                b = c // CB
                nc.scalar.activation(dst[:].rearrange("p (q t) -> p t q", t=TB),
                                     misc[:].rearrange("p (t q) -> p t q", t=TB), ACT.Identity,
                                     scale=mod_sb[:, b, which + 1:which + 2],
                                     bias=mod_sb[:, b, which:which + 1]).then_inc(s_done, 1)
                act.wait_ge(s_done, c + 1)
                act.sem_inc(misc_drained, 1)

            def pre_h(c, k):
                turned(c, k, 0, h1, h1_ready)

            def post_h(c, k):
                if not is_first(c):
                    act.wait_ge(h2_ready, c)
                turned(c, k, 3, h2, h2_full)

            def take_xs(c, k, hf):
                act.wait_ge(misc_filled, k + 1)
                if not (is_first(c) and hf == 0):
                    act.wait_ge(conv_done, HALVES * c + hf)
                nc.scalar.activation(xs_ext[:, K - 1:], misc[:], ACT.Copy).then_inc(xs_ready, 1)
                act.wait_ge(xs_ready, HALVES * c + hf + 1)
                act.sem_inc(misc_drained, 1)

            def silu_xc(c, hf):
                act.wait_ge(conv_done, HALVES * c + hf + 1)
                nc.scalar.activation(xc[:, hf, :], xc[:, hf, :], ACT.Silu).then_inc(xc_ready, 1)

            def softplus(c, k, hf):
                act.wait_ge(misc_filled, k + 1)
                bias = cols[:, hf, K + 1:K + 2]
                nc.scalar.activation(delta[:, hf, :], misc[:], ACT.Relu, bias=bias)
                if not is_first(c):
                    act.wait_ge(delta_ready, HALVES * c)
                nc.scalar.activation(log_part[:, hf, :], misc[:], ACT.Abs, bias=bias).then_inc(sp_step, 1)
                act.wait_ge(sp_step, 2 * (HALVES * c + hf) + 1)
                act.sem_inc(misc_drained, 1)
                nc.scalar.activation(log_part[:, hf, :], log_part[:, hf, :], ACT.Exp, scale=-1.0).then_inc(sp_step, 1)
                act.wait_ge(sp_step, 2 * (HALVES * c + hf) + 2)
                nc.scalar.activation(log_part[:, hf, :], log_part[:, hf, :], ACT.Ln, bias=1.0).then_inc(sp_ready, 1)

            def exps(c, j):
                for hf in range(HALVES):
                    u = HALVES * j + hf
                    act.wait_ge(delta_ready, HALVES * c + HALVES)
                    if is_first(c) and u < SLOTS:
                        act.wait_ge(lo_done, u + 1)
                    else:
                        act.wait_ge(unit_reduced, UNITS * c + u - SLOTS + 1)
                    for m in range(2):
                        n = 2 * j + m
                        last = nc.scalar.activation(ring[:, u % SLOTS, m, :], delta[:, hf, :], ACT.Exp,
                                                    scale=a_neg[:, hf, n:n + 1])
                    last.then_inc(exp_done, 1)

            def silu_gate(c, k, hf):
                act.wait_ge(misc_filled, k + 1)
                nc.scalar.activation(gate[:, hf, :], misc[:], ACT.Silu).then_inc(gate_ready, 1)
                act.wait_ge(gate_ready, HALVES * c + hf + 1)
                act.sem_inc(misc_drained, 1)

            def silu_g(c, b):
                act.wait_ge(g_ready, NB * c + b + 1)
                nc.scalar.activation(p_tile[:, b % BLOCKS, :], g_bank[b % 2][:], ACT.Silu).then_inc(silu_done, 1)

            def ffn_out(c, h2_split):
                act.wait_ge(acc_ready, c + 1)
                act.wait_ge(h2_ready, h2_split)
                nc.scalar.activation(f_t[:], acc[:], ACT.Identity, scale=mod_sb[:, c // CB, 5:6]).then_inc(ft_ready, 1)

            act.wait_ge(small_in, 16 * 8)
            nc.scalar.activation(sc[:], c_sb[:], ACT.Silu).then_inc(act_set, 1)
            nc.scalar.activation(a_neg[:], a_neg[:], ACT.Exp).then_inc(act_set, 1)
            act.wait_ge(act_set, 2)
            nc.scalar.activation(a_neg[:], a_neg[:], ACT.Copy, scale=-1.0).then_inc(act_set, 1)
            for e in range(NE):
                act.wait_ge(gu_in, 16 * (e + 1))
                nc.scalar.activation(gu_hi[:, e], ring[:, e], ACT.Copy).then_inc(hi_done, 1)
            act.wait_ge(dve_set, 10)
            act.wait_ge(act_set, 3)
            pre_h(0, 0)
            take_xs(0, 1, 0)
            take_xs(0, 2, 1)
            silu_xc(0, 0)
            silu_xc(0, 1)
            softplus(0, 4, 0)
            softplus(0, 5, 1)
            exps(0, 0)
            exps(0, 1)

            def body(i, pre=True, ffn=True):
                for part in range(PARTS):
                    if part < 3:
                        exps(i, 2 * part + 2)
                        exps(i, 2 * part + 3)
                        if part == 2 and pre:
                            act.wait_ge(exp_done, UNITS * (i + 1))
                            softplus(i + 1, misc_pre(i, 4), 0)
                            softplus(i + 1, misc_pre(i, 5), 1)
                    elif pre:
                        exps(i + 1, 0)
                        exps(i + 1, 1)
                    for k in range(BLOCKS):
                        if ffn:
                            silu_g(i - 1, part * BLOCKS + k)
                        if part == 0 and k in (1, 3):
                            silu_gate(i, misc_post(i, k // 2), k // 2)
                        if part == 1 and pre and k in (2, 4):
                            silu_xc(i + 1, k // 2 - 1)
                    if part == 0 and pre:
                        pre_h(i + 1, misc_pre(i, 0))
                        take_xs(i + 1, misc_pre(i, 1), 0)
                        take_xs(i + 1, misc_pre(i, 2), 1)
                    if part == 3:
                        post_h(i, misc_post(i, 3))
                if ffn:
                    ffn_out(i - 1, i + 1)

            body(0, ffn=False)
            with act.Fori(1, NC - 1) as i:
                body(i)
            body(NC - 1, pre=False)
            for b in range(NB):
                silu_g(NC - 1, b)
            ffn_out(NC - 1, NC)

        @block.vector
        def _(dve):
            def norm(which, c, src, dst):
                step, base = ln_step[which], 4 * c
                stats, mv = ln_in[:, which], ln_mv[:, which]
                for t in range(TB):
                    last = nc.vector.bn_stats(stats[:, t, :], src(t))
                last.then_inc(step, 1)
                dve.wait_ge(step, base + 1)
                dve.sem_inc(step, 1)
                for t in range(TB):
                    last = nc.vector.bn_aggr(mv[:, t, :], stats[:, t, :])
                last.then_inc(step, 1)
                dve.wait_ge(step, base + 3)
                nc.vector.tensor_scalar(ln_ve[:, which, :], mv[:, :, 1], EPS, None, ALU.add).then_inc(step, 1)
                dve.wait_ge(ln_ready[which], c + 1)
                for t in range(TB):
                    last = nc.vector.tensor_scalar(dst(t), src(t), mv[:, t, 0:1], ln_rstd[:, which, t:t + 1],
                                                   ALU.subtract, ALU.mult)
                last.then_inc(xn_ready[which], 1)

            def pre_norm(c):
                dve.wait_ge(x_loaded, 16 * (c + 1))
                norm(0, c, lambda t: tok[:, t, :], lambda t: tok[:, t, :])

            def conv(c, hf):
                n_step, n_halo = (K - 1) * (HALVES * c + hf), 2 * (HALVES * c + hf)
                nc.vector.tensor_copy(xs_ext[:, 0:K - 1], halo[:, c % CB, hf, :]).then_inc(halo_in, 1)
                dve.wait_ge(halo_in, n_halo + 1)
                dve.wait_ge(xs_ready, HALVES * c + hf + 1)
                nc.vector.tensor_copy(halo[:, c % CB + 1, hf, :], xs_ext[:, L:]).then_inc(halo_in, 1)
                nc.vector.tensor_scalar(xc[:, hf, :], xs_ext[:, K - 1:], cols[:, hf, K - 1:K], cols[:, hf, K:K + 1],
                                        ALU.mult, ALU.add).then_inc(conv_step, 1)
                for k in range(K - 1):
                    dve.wait_ge(conv_step, n_step + k + 1)
                    nc.vector.scalar_tensor_tensor(out=xc[:, hf, :], in0=xs_ext[:, k:k + L],
                                                   scalar=cols[:, hf, k:k + 1], in1=xc[:, hf, :], op0=ALU.mult,
                                                   op1=ALU.add).then_inc(conv_step if k < K - 2 else conv_done, 1)
                dve.wait_ge(halo_in, n_halo + 2)
                dve.wait_ge(conv_done, HALVES * c + hf + 1)

            def take_xdbl(c, k):
                dve.wait_ge(misc_filled, k + 1)
                if not is_first(c):
                    dve.wait_ge(bc_stored, 16 * c)
                nc.vector.tensor_copy(x_dbl[0:R + 2 * N, :], misc[0:R + 2 * N, :]).then_inc(xdbl_ready, 1)
                dve.wait_ge(xdbl_ready, c + 1)
                dve.sem_inc(misc_drained, 1)

            def finish_delta(c, hf):
                dve.wait_ge(sp_ready, HALVES * c + hf + 1)
                nc.vector.tensor_tensor(delta[:, hf, :], delta[:, hf, :], log_part[:, hf, :], ALU.add).then_inc(delta_ready, 1)

            def take_du(c, hf):
                dve.wait_ge(delta_ready, HALVES * c + hf + 1)
                nc.vector.tensor_tensor(du[:, hf, :], delta[:, hf, :], xc[:, hf, :], ALU.mult).then_inc(du_ready, 1)

            def dbu(c, j, hf, m):
                if m == 0:
                    dve.wait_ge(b_loaded[j % 2], 16 * (PAIRS // 2 * c + j // 2 + 1))
                    dve.wait_ge(du_ready, HALVES * c + HALVES)
                if not (is_first(c) and j == 0 and hf == 0):
                    dve.wait_ge(scan_step, 2 * N * c + 2 * (HALVES * j + hf) + m - 1)
                nc.vector.tensor_tensor(dbu_bank[m][:], du[:, hf, :], b_tile[:, j % 2, m, :],
                                        ALU.mult).then_inc(dbu_done, 1)

            def scan(c, j, hf, m):
                u = HALVES * j + hf
                if m == 0:
                    dve.wait_ge(exp_done, UNITS * c + u + 1)
                dve.wait_ge(dbu_done, 2 * N * c + 2 * u + m + 1)
                n = 2 * j + m
                h = ring[:, u % SLOTS, m, :]
                nc.vector.tensor_tensor_scan(h, h, dbu_bank[m][:], carry[:, c % CB, hf, n:n + 1], ALU.mult,
                                             ALU.add).then_inc(scan_step, 1)

            def keep_carry(c, j, hf):
                u = HALVES * j + hf
                dve.wait_ge(scan_step, 2 * N * c + 2 * u + 2)
                nc.vector.tensor_copy(carry[:, c % CB + 1, hf, 2 * j:2 * j + 2],
                                      ring[:, u % SLOTS, :, L - 1]).then_inc(scan_done, 1)

            def times_u(c, b):
                dve.wait_ge(silu_done, NB * c + b + 1)
                dve.wait_ge(u_ready, NB * c + b + 1)
                p = p_tile[:, b % BLOCKS, :]
                nc.vector.tensor_tensor(p, u_bank[b % 2][:], p, ALU.mult).then_inc(p_ready, 1)

            def residual(c, k):
                dve.wait_ge(misc_filled, k + 1)
                dve.wait_ge(xres_loaded, 16 * (c + 1))
                t = x1[:, c % 2].rearrange("p t h -> p (t h)")
                nc.vector.tensor_tensor(t, misc[:], t, ALU.add).then_inc(x1_ready, 1)
                dve.wait_ge(x1_ready, c + 1)
                dve.sem_inc(misc_drained, 1)

            def post_norm(c):
                norm(1, c, lambda t: x1[:, c % 2, t, :], lambda t: tok2[:, t, :])

            def split_h2(c):
                dve.wait_ge(h2_full, c + 1)
                nc.vector.tensor_copy(h2_hi[:], h2[:]).then_inc(h2_step, 1)
                dve.wait_ge(h2_step, c + 1)
                nc.vector.tensor_tensor(h2_lo[:], h2[:], h2_hi[:].bitcast(F32), ALU.subtract).then_inc(h2_ready, 1)

            def add_ffn(c):
                dve.wait_ge(ft_turned, c + 1)
                t = x1[:, c % 2].rearrange("p t h -> p (t h)")
                nc.vector.tensor_tensor(t, acc[:], t, ALU.add).then_inc(out_ready, 1)

            nc.vector.memset(halo[:], 0.0).then_inc(dve_set, 1)
            nc.vector.memset(carry[:], 0.0).then_inc(dve_set, 1)
            nc.vector.memset(sc_wide[:], 1.0).then_inc(dve_set, 1)
            dve.wait_ge(act_set, 1)
            dve.wait_ge(dve_set, 3)
            for b in range(B):
                last = nc.vector.tensor_scalar(sc_wide[:, b, :], sc_wide[:, b, :], sc[:, b:b + 1], None, ALU.mult)
            last.then_inc(dve_set, 1)
            pre_norm(0)
            dve.wait_ge(pe_set, 1)
            nc.vector.tensor_copy(mod_sb[:], acc[:, 0:6 * B].rearrange("p (k b) -> p b k", b=B)).then_inc(dve_set, 1)
            dve.wait_ge(dve_set, 5)
            for k in (1, 4):
                last = nc.vector.tensor_scalar(mod_sb[:, :, k], mod_sb[:, :, k], 1.0, None, ALU.add)
            last.then_inc(dve_set, 1)

            def clamp(v, sign, count):
                nc.vector.tensor_scalar(sign, v, 0.0, 2.0, ALU.is_ge, ALU.mult).then_inc(dve_set, 1)
                dve.wait_ge(dve_set, count + 1)
                nc.vector.tensor_scalar(sign, sign, -1.0, None, ALU.add).then_inc(dve_set, 1)
                dve.wait_ge(dve_set, count + 2)
                nc.vector.tensor_tensor(v, v, sign, ALU.mult).then_inc(dve_set, 1)
                dve.wait_ge(dve_set, count + 3)
                nc.vector.scalar_tensor_tensor(out=v, in0=v, scalar=0.25, in1=sign, op0=ALU.max,
                                               op1=ALU.mult).then_inc(dve_set, 1)
                dve.wait_ge(dve_set, count + 4)

            clamp(mod_sb[:, :, 5], gb_sign[:], 6)
            dve.wait_ge(pe_set, 2)
            nc.vector.tensor_copy(ga_row[:], u_bank[0][:, 0:B * H].rearrange("p (b h) -> p b h", b=B)).then_inc(dve_set, 1)
            dve.wait_ge(dve_set, 11)
            clamp(ga_row[:], ga_sign[:], 11)
            for b in range(B):
                for hf in range(HALVES):
                    last = nc.vector.tensor_tensor(w_out_ga[:, b, hf, :], w_out_sb[:, hf, :], ga_row[:, b, :], ALU.mult)
            last.then_inc(dve_set, 1)
            dve.wait_ge(dve_set, 16)
            conv(0, 0)
            conv(0, 1)
            take_xdbl(0, 3)
            for hf in range(HALVES):
                finish_delta(0, hf)
                take_du(0, hf)

            def units(c, j, mults, late):
                for hf in range(HALVES):
                    dbu(c, j, hf, 0)
                    if late:
                        late.pop(0)()
                    if mults:
                        mults.pop(0)()
                    dbu(c, j, hf, 1)
                    if mults:
                        mults.pop(0)()
                    scan(c, j, hf, 0)
                    if mults:
                        mults.pop(0)()
                    scan(c, j, hf, 1)
                    if mults:
                        mults.pop(0)()
                    late.append(lambda c=c, j=j, hf=hf: keep_carry(c, j, hf))

            first = []
            units(0, 0, [], first)
            units(0, 1, [], first)
            first.pop(0)()

            def body(i, pre=True, ffn=True):
                for part in range(PARTS):
                    late = []
                    mults = [lambda b=b: times_u(i - 1, b) for b in range(part * BLOCKS, (part + 1) * BLOCKS)] if ffn else []
                    c, j = (i, 2 * part + 2) if part < 3 else (i + 1, 0)
                    if part == 3 and pre:
                        for hf in range(HALVES):
                            take_du(i + 1, hf)
                        dve.wait_ge(scan_done, UNITS * (i + 1))
                    if part < 3 or pre:
                        if part == 2 and pre:
                            units(c, j, [], late)
                            finish_delta(i + 1, 0)
                            finish_delta(i + 1, 1)
                        else:
                            units(c, j, mults, late)
                        if part == 0 and pre:
                            late.pop(0)()
                            pre_norm(i + 1)
                        if part == 1 and pre:
                            take_xdbl(i + 1, misc_pre(i, 3))
                        units(c, j + 1, mults, late)
                        while late:
                            late.pop(0)()
                    while mults:
                        mults.pop(0)()
                    if part == 0 and pre:
                        conv(i + 1, 0)
                        conv(i + 1, 1)
                    if part == 3:
                        residual(i, misc_post(i, 2))
                        post_norm(i)
                        split_h2(i)
                if ffn:
                    add_ffn(i - 1)

            body(0, ffn=False)
            with dve.Fori(1, NC - 1) as i:
                body(i)
            body(NC - 1, pre=False)
            for b in range(NB):
                times_u(NC - 1, b)
            add_ffn(NC - 1)

        @block.gpsimd
        def _(pool):
            def rstd(which, c):
                pool.wait_ge(ln_step[which], 4 * (c + 1))
                nc.gpsimd.tensor_tensor(ln_rstd[:, which, :], ln_ve[:, which, :], minus_half[:],
                                        ALU.pow).then_inc(ln_ready[which], 1)

            def reduce_unit(c, j, hf):
                u = HALVES * j + hf
                step = 2 * (UNITS * c + u)
                pool.wait_ge(scan_done, UNITS * c + u + 1)
                if hf == 0:
                    pool.wait_ge(c_loaded[j % 4], 16 * (PAIRS // 4 * c + j // 4 + 1))
                hc = ring[:, u % SLOTS]
                nc.gpsimd.tensor_tensor(hc, hc, c_tile[:, j % 4], ALU.mult).then_inc(pool_step, 1)
                pool.wait_ge(pool_step, step + 1)
                if j == 0:
                    nc.gpsimd.tensor_tensor(y[:, hf, :], hc[:, 0, :], hc[:, 1, :], ALU.add).then_inc(unit_reduced, 1)
                    pool.sem_inc(pool_step, 1)
                else:
                    nc.gpsimd.tensor_tensor(hc[:, 0, :], hc[:, 0, :], hc[:, 1, :], ALU.add).then_inc(pool_step, 1)
                    pool.wait_ge(pool_step, step + 2)
                    pool.wait_ge(unit_reduced, UNITS * c + u - 1)
                    nc.gpsimd.tensor_tensor(y[:, hf, :], y[:, hf, :], hc[:, 0, :], ALU.add).then_inc(unit_reduced, 1)

            def gated(c):
                pool.wait_ge(unit_reduced, UNITS * (c + 1))
                pool.wait_ge(gate_ready, HALVES * (c + 1))
                for hf in range(HALVES):
                    nc.gpsimd.tensor_tensor(gate[:, hf, :], gate[:, hf, :], y[:, hf, :], ALU.mult).then_inc(r_ready, 1)

            nc.gpsimd.memset(minus_half[:], -0.5).then_inc(pool_set, 1)
            nc.gpsimd.memset(ident[:], 0.0).then_inc(pool_set, 1)
            pool.wait_ge(pool_set, 2)
            nc.gpsimd.affine_select(out=ident[:], in_=ident[:], compare_op=ALU.not_equal, fill=1.0, base=0,
                                    pattern=[[-1, P]], channel_multiplier=1).then_inc(pool_set, 1)
            rstd(0, 0)
            for e in range(NE):
                pool.wait_ge(hi_done, e + 1)
                nc.gpsimd.tensor_tensor(gu_lo[:, e], ring[:, e], gu_hi[:, e].bitcast(F32),
                                        ALU.subtract).then_inc(lo_done, 1)
            for j in range(2):
                for hf in range(HALVES):
                    reduce_unit(0, j, hf)

            def body(i, pre=True):
                for part in range(PARTS):
                    c, j = (i, 2 * part + 2) if part < 3 else (i + 1, 0)
                    if part == 3:
                        gated(i)
                    for k in range(2):
                        if part < 3 or pre:
                            for hf in range(HALVES):
                                reduce_unit(c, j + k, hf)
                        if part == 0 and k == 0 and pre:
                            rstd(0, i + 1)
                        if part == 3 and k == 0:
                            rstd(1, i)

            with pool.Fori(0, NC - 1) as i:
                body(i)
            body(NC - 1, pre=False)


def kernel(**inputs):
    import numpy as np
    import concourse.bacc as bacc
    from concourse.bass_utils import run_bass_kernel_spmd

    a = {k: np.asarray(v) for k, v in inputs.items()}

    def halves(t):
        return t.reshape(HALVES, P, -1).transpose(1, 0, 2)

    cols = np.concatenate([halves(a["L0_attn_conv_w"].reshape(D, K)), halves(a["L0_attn_conv_b"].reshape(D, 1)),
                           halves(a["L0_attn_b_dt"].reshape(D, 1))], axis=2)
    gu = np.stack([a["L0_ffn_Wg"], a["L0_ffn_Wu"]], axis=2)
    arrays = {
        "x": a["L0_attn_x"].reshape(NC * P, TB * H),
        "w_in": a["L0_attn_W_in"].T,
        "cols": cols,
        "w_x": halves(a["L0_attn_W_x"].T),
        "w_dt": a["L0_attn_W_dt"].T,
        "a_log": halves(a["L0_attn_A_log"]),
        "w_out": halves(a["L0_attn_W_out"].T),
        "w_gu": gu.transpose(1, 0, 2, 3),
        "w_d": a["L0_ffn_Wd"].reshape(NB, P, H).transpose(1, 0, 2),
        "c_t": a["L0_c"].T,
        "w_mod": a["L0_wmod"],
    }
    arrays = {k: np.ascontiguousarray(v) for k, v in arrays.items()}
    nc = bacc.Bacc("TRN2", target_bir_lowering=False, num_devices=1)
    t = {k: nc.dram_tensor("in_" + k, v.shape, F32, kind="ExternalInput").ap() for k, v in arrays.items()}
    out = nc.dram_tensor("out_tokens", (NC * P, TB * H), F32, kind="ExternalOutput").ap()
    bc_dram = nc.dram_tensor("bc_rows", (NC * 2 * N, L), F32, kind="Internal").ap()
    build(nc, t["x"], t["w_in"], t["cols"], t["w_x"], t["w_dt"], t["a_log"], t["w_out"], t["w_gu"],
          t["w_d"], t["c_t"], t["w_mod"], out, bc_dram)
    r = run_bass_kernel_spmd(nc, [{"in_" + k: v for k, v in arrays.items()}], core_ids=[0])
    return r.results[0]["out_tokens"].reshape(B, S, H)
```

```python
from contextlib import ExitStack

import concourse.bass as bass
from concourse import mybir

F32 = mybir.dt.float32
F32R = mybir.dt.float32r
ALU = mybir.AluOpType
ACT = mybir.ActivationFunctionType

P = 128
B, S, H = 2, 2048, 128
D, N, R, K = 256, 16, 64, 4
NE, F = 8, 512
L = 512
NC = B * S // L
CB = S // L
HALVES = D // P
PAIRS = N // 2
UNITS = PAIRS * HALVES
TB = L // P
FB = F // P
NB = NE * FB
PARTS = 4
BLOCKS = NB // PARTS
SLOTS = 8
EPS = 1e-5
EXP_LN = "natural_log_exp_and_others"
MISC_PRE, MISC_POST = 6, 4
MISC = MISC_PRE + MISC_POST


def is_first(c):
    return isinstance(c, int) and c == 0


def build(nc, x, w_in, cols_in, w_x, w_dt, a_log, w_out, w_gu, w_d, c_t, w_mod, out, bc_dram):
    with ExitStack() as ctx:
        def sb(name, shape, dt=F32):
            return ctx.enter_context(nc.sbuf_tensor(name, shape, dt))

        def bank(name):
            return ctx.enter_context(nc.psum_tensor(name, [P, 512], F32))

        def sem(name):
            return ctx.enter_context(nc.semaphore(name))

        gu_hi = sb("gu_hi", [P, NE, 2, F], F32R)
        gu_lo = sb("gu_lo", [P, NE, 2, F], F32R)
        wd = sb("wd", [P, NB, H])
        w_in_sb = sb("w_in_sb", [P, 2 * D])
        w_x_sb = sb("w_x_sb", [P, HALVES, R + 2 * N])
        w_dt_sb = sb("w_dt_sb", [R, D])
        w_out_ga = sb("w_out_ga", [P, B, HALVES, H])
        cols = sb("cols", [P, HALVES, K + 2])
        a_neg = sb("a_neg", [P, HALVES, N])
        ident = sb("ident", [P, P])
        c_sb = sb("c_sb", [P, B])
        sc = sb("sc", [P, B])
        mod_sb = sb("mod_sb", [P, B, 6])
        gb_sign = sb("gb_sign", [P, B])
        minus_half = sb("minus_half", [P, TB])
        tok_z = sb("tok_z", [P, 2, L])
        tok, tok2 = (tok_z[:, k].rearrange("p (t h) -> p t h", t=TB) for k in range(2))
        ln_in = sb("ln_in", [P, 2, TB, 6])
        ln_mv = sb("ln_mv", [P, 2, TB, 2])
        ln_ve = sb("ln_ve", [P, 2, TB])
        ln_rstd = sb("ln_rstd", [P, 2, TB])
        h1 = sb("h1", [P, L])
        xs_ext = sb("xs_ext", [P, HALVES, K - 1 + L])
        halo = sb("halo", [P, CB + 1, HALVES, K - 1])
        xc = sb("xc", [P, HALVES, L])
        x_dbl = sb("x_dbl", [P, L])
        log_part = sb("log_part", [P, HALVES, L])
        delta = sb("delta", [P, HALVES, L])
        du = sb("du", [P, HALVES, L])
        ring = sb("ring", [P, SLOTS, 2, L])
        b_tile = sb("b_tile", [P, 2, 2, L])
        c_tile = sb("c_tile", [P, 4, 2, L])
        carry = sb("carry", [P, CB + 1, HALVES, N])
        y = sb("y", [P, HALVES, L])
        gate = sb("gate", [P, HALVES, L])
        x1 = sb("x1", [P, 2, TB, H])
        h2 = sb("h2", [P, L])
        h2_hi = sb("h2_hi", [P, L], F32R)
        h2_lo = sb("h2_lo", [P, L], F32R)
        p_tile = sb("p_tile", [P, BLOCKS, L])
        sc_wide, ga_row, ga_sign, w_out_sb = (p_tile[:, k, 0:2 * P].rearrange("p (b h) -> p b h", b=2) for k in range(4))
        f_t = xs_ext[:, 0, 0:L]

        g_bank = [bank("g0"), bank("g1")]
        u_bank = [bank("u0"), bank("u1")]
        acc = bank("acc")
        dbu_bank = [bank("dbu0"), bank("dbu1")]
        misc = bank("misc")

        small_in, gu_in, wd_in = sem("small_in"), sem("gu_in"), sem("wd_in")
        dve_set, act_set, pe_set, pool_set = sem("dve_set"), sem("act_set"), sem("pe_set"), sem("pool_set")
        hi_done, lo_done = sem("hi_done"), sem("lo_done")
        x_loaded, xres_loaded, out_stored, bc_stored = sem("x_loaded"), sem("xres_loaded"), sem("out_stored"), sem("bc_stored")
        b_loaded = [sem(f"b_loaded{i}") for i in range(2)]
        c_loaded = [sem(f"c_loaded{i}") for i in range(4)]
        bc_seen = sem("bc_seen")
        misc_filled, misc_drained = sem("misc_filled"), sem("misc_drained")
        ln_step = [sem("ln1_step"), sem("ln2_step")]
        ln_ready = [sem("ln1_ready"), sem("ln2_ready")]
        xn_ready = [sem("xn1_ready"), sem("xn2_ready")]
        h1_ready, xs_ready, halo_in, conv_step, conv_done, xc_ready = (
            sem("h1_ready"), sem("xs_ready"), sem("halo_in"), sem("conv_step"), sem("conv_done"), sem("xc_ready"))
        xdbl_ready, z_ready, sp_step, sp_ready, delta_ready, du_ready = (
            sem("xdbl_ready"), sem("z_ready"), sem("sp_step"), sem("sp_ready"), sem("delta_ready"), sem("du_ready"))
        exp_done, dbu_done, scan_step, scan_done, pool_step, unit_reduced = (
            sem("exp_done"), sem("dbu_done"), sem("scan_step"), sem("scan_done"), sem("pool_step"), sem("unit_reduced"))
        gate_ready, r_ready, x1_ready, h2_full, h2_step, h2_ready = (
            sem("gate_ready"), sem("r_ready"), sem("x1_ready"), sem("h2_full"), sem("h2_step"), sem("h2_ready"))
        g_ready, u_ready, silu_done, p_ready, acc_ready, ft_ready, ft_turned, out_ready = (
            sem("g_ready"), sem("u_ready"), sem("silu_done"), sem("p_ready"), sem("acc_ready"), sem("ft_ready"),
            sem("ft_turned"), sem("out_ready"))

        def chunk_rows(t, c):
            return t[bass.ts(c, P), :]

        def misc_pre(i, k):
            return k if isinstance(i, int) and i < 0 else MISC_PRE + MISC * i + 2 + k

        def misc_post(i, k):
            last = 0 if isinstance(i, int) and i == NC - 1 else MISC_PRE
            return MISC_PRE + MISC * i + k + (last if k >= 2 else 0)

        block = ctx.enter_context(nc.Block())

        @block.sync
        def _(sp):
            def load_x(c):
                if not is_first(c):
                    sp.wait_ge(delta_ready, HALVES * c)
                sp.dma_start(tok_z[:, 0], chunk_rows(x, c)).then_inc(x_loaded, 16)

            def load_residual(c, stored):
                if stored is not None:
                    sp.wait_ge(out_stored, stored)
                sp.dma_start(x1[:, c % 2].rearrange("p t h -> p (t h)"), chunk_rows(x, c)).then_inc(xres_loaded, 16)

            def store_bc(c):
                sp.wait_ge(xdbl_ready, c + 1)
                sp.dma_start(bc_dram[bass.ts(c, 2 * N), :], x_dbl[R:R + 2 * N, :]).then_inc(bc_stored, 16)

            def load_pair(c, j):
                if j == 0:
                    sp.wait_ge(bc_stored, 16 * (c + 1))
                    sp.sem_inc(bc_seen, 1)
                def rows(first):
                    return bc_dram[bass.ds(2 * N * c + first + 2 * j, 2), :].partition_broadcast(P)
                if not (is_first(c) and j < 2):
                    sp.wait_ge(dbu_done, 2 * N * c + 4 * (j - 1))
                sp.dma_start(b_tile[:, j % 2], rows(0)).then_inc(b_loaded[j % 2], 16)
                if not (is_first(c) and j < 4):
                    sp.wait_ge(unit_reduced, UNITS * c + 2 * (j - 3))
                sp.dma_start(c_tile[:, j % 4], rows(N)).then_inc(c_loaded[j % 4], 16)

            def store_out(c):
                sp.wait_ge(out_ready, c + 1)
                sp.dma_start(chunk_rows(out, c), x1[:, c % 2].rearrange("p t h -> p (t h)")).then_inc(out_stored, 16)

            load_x(0)
            for dst, src in ((c_sb, c_t), (w_in_sb, w_in), (cols, cols_in), (w_x_sb, w_x), (w_dt_sb, w_dt),
                             (a_neg, a_log)):
                sp.dma_start(dst[:], src).then_inc(small_in, 16)
            sp.dma_start(w_out_sb, w_out).then_inc(small_in, 16)
            sp.dma_start(b_tile[:].rearrange("p a b l -> p (a b l)")[:, 0:6 * H], w_mod).then_inc(small_in, 16)
            for e in range(NE):
                sp.dma_start(ring[:, e], w_gu[:, e]).then_inc(gu_in, 16)
                sp.wait_ge(gu_in, 16 * (e + 1))
            load_residual(0, None)
            sp.dma_start(wd[:], w_d).then_inc(wd_in, 16)
            store_bc(0)
            sp.wait_ge(pe_set, 2)
            load_pair(0, 0)
            load_pair(0, 1)

            def body(i, pre=True, late=True):
                if pre:
                    load_x(i + 1)
                load_pair(i, 2)
                load_pair(i, 3)
                if late:
                    store_out(i - 2)
                    load_residual(i, 16 * (i - 1))
                load_pair(i, 4)
                load_pair(i, 5)
                if pre:
                    store_bc(i + 1)
                load_pair(i, 6)
                load_pair(i, 7)
                if pre:
                    load_pair(i + 1, 0)
                    load_pair(i + 1, 1)

            body(0, late=False)
            load_residual(1, None)
            body(1, late=False)
            with sp.Fori(2, NC - 1) as i:
                body(i)
            body(NC - 1, pre=False)
            store_out(NC - 2)
            store_out(NC - 1)
            sp.wait_ge(out_stored, 16 * NC)
            sp.wait_ge(bc_stored, 16 * NC)

        @block.tensor
        def _(pe):
            def use_misc(k):
                if not is_first(k):
                    pe.wait_ge(misc_drained, k)

            def turn(dst, src, s_done):
                for t in range(TB):
                    last = nc.tensor.transpose(dst(t), src(t), ident[:])
                last.then_inc(s_done, 1)

            def pre_turn(c, k):
                use_misc(k)
                pe.wait_ge(xn_ready[0], c + 1)
                turn(lambda t: misc[:, t * P:(t + 1) * P], lambda t: tok[:, t, :], misc_filled)

            def in_proj(c, k, block_):
                use_misc(k)
                pe.wait_ge(h1_ready, c + 1)
                nc.tensor.matmul(misc[:], w_in_sb[:, block_ * P:(block_ + 1) * P], h1[:], start=True,
                                 stop=True).then_inc(misc_filled, 1)

            def x_proj(c, k):
                use_misc(k)
                pe.wait_ge(xc_ready, 2 * c + 2)
                for hf in range(HALVES):
                    last = nc.tensor.matmul(misc[0:R + 2 * N, :], w_x_sb[:, hf, :], xc[:, hf, :],
                                            start=(hf == 0), stop=(hf == 1))
                last.then_inc(misc_filled, 1)

            def dt_proj(c, k, hf):
                use_misc(k)
                pe.wait_ge(xdbl_ready, c + 1)
                nc.tensor.matmul(misc[:], w_dt_sb[:, hf * P:(hf + 1) * P], x_dbl[0:R, :], start=True,
                                 stop=True).then_inc(misc_filled, 1)

            def out_proj(c, k):
                use_misc(k)
                pe.wait_ge(r_ready, 2 * c + 2)
                for t in range(TB):
                    for hf in range(HALVES):
                        r_t = gate[:, hf, :].rearrange("p (q t) -> p t q", t=TB)[:, t, :]
                        last = nc.tensor.matmul(misc[:, t * P:(t + 1) * P], r_t, w_out_ga[:, c // CB, hf, :],
                                                start=(hf == 0), stop=(hf == 1))
                last.then_inc(misc_filled, 1)

            def post_turn(c, k):
                use_misc(k)
                pe.wait_ge(xn_ready[1], c + 1)
                turn(lambda t: misc[:, t * P:(t + 1) * P], lambda t: tok2[:, t, :], misc_filled)

            def gate_up(c, b):
                e, f = b // FB, (b % FB) * P
                if b == 0:
                    pe.wait_ge(h2_ready, c + 1)
                for which, to, used, s_done in ((0, g_bank, silu_done, g_ready), (1, u_bank, p_ready, u_ready)):
                    if b % BLOCKS >= 2:
                        pe.wait_ge(used, NB * c + b - 1)
                    w_hi, w_lo = gu_hi[:, e, which, f:f + P], gu_lo[:, e, which, f:f + P]
                    nc.tensor.matmul(to[b % 2][:], w_hi, h2_hi[:], start=True, stop=False)
                    nc.tensor.matmul(to[b % 2][:], w_hi, h2_lo[:], start=False, stop=False)
                    nc.tensor.matmul(to[b % 2][:], w_lo, h2_hi[:], start=False, stop=True).then_inc(s_done, 1)

            def down(c, b):
                pe.wait_ge(p_ready, NB * c + b + 1)
                last = nc.tensor.matmul(acc[:], wd[:, b, :], p_tile[:, b % BLOCKS, :], start=(b == 0),
                                        stop=(b == NB - 1))
                if b == NB - 1:
                    last.then_inc(acc_ready, 1)

            def ffn_tail(c):
                pe.wait_ge(ft_ready, c + 1)
                turn(lambda t: acc[:, t * P:(t + 1) * P],
                     lambda t: f_t.rearrange("p (q t) -> p t q", t=TB)[:, t, :], ft_turned)

            pe.wait_ge(small_in, 16 * 8)
            pe.wait_ge(act_set, 1)
            w_mod_sb = b_tile[:].rearrange("p a b l -> p (a b l)")[:, 0:6 * H]
            for k in range(6):
                last = nc.tensor.matmul(acc[:, B * k:B * k + B], w_mod_sb[:, k * H:(k + 1) * H], sc[:], start=True,
                                        stop=True)
            last.then_inc(pe_set, 1)
            pe.wait_ge(dve_set, 4)
            for b in range(B):
                last = nc.tensor.matmul(u_bank[0][:, b * H:(b + 1) * H], sc_wide[:, b, :],
                                        w_mod_sb[:, 2 * H:3 * H], start=True, stop=True)
            last.then_inc(pe_set, 1)
            pe.wait_ge(pool_set, 2)
            pre_turn(0, 0)
            in_proj(0, 1, 0)
            in_proj(0, 2, 1)
            x_proj(0, 3)
            dt_proj(0, 4, 0)
            dt_proj(0, 5, 1)

            def body(i, pre=True, ffn=True):
                tasks = {}
                tasks[0, -1] = lambda: in_proj(i, misc_post(i, 0), 2)
                tasks[0, 0] = lambda: in_proj(i, misc_post(i, 1), 3)
                if pre:
                    tasks[0, 2] = lambda: pre_turn(i + 1, misc_pre(i, 0))
                    tasks[0, 4] = lambda: in_proj(i + 1, misc_pre(i, 1), 0)
                    tasks[0, 6] = lambda: in_proj(i + 1, misc_pre(i, 2), 1)
                    tasks[1, 3] = lambda: x_proj(i + 1, misc_pre(i, 3))
                    tasks[1, 6] = lambda: dt_proj(i + 1, misc_pre(i, 4), 0)
                    tasks[1, 8] = lambda: dt_proj(i + 1, misc_pre(i, 5), 1)
                tasks[3, 5] = lambda: out_proj(i, misc_post(i, 2))
                tasks[3, 13] = lambda: post_turn(i, misc_post(i, 3))
                for part in range(PARTS):
                    for k in range(-1, 2 * BLOCKS):
                        if ffn and k >= 0:
                            (gate_up if k < BLOCKS else down)(i - 1, part * BLOCKS + k % BLOCKS)
                        if (part, k) in tasks:
                            tasks[part, k]()
                if ffn:
                    ffn_tail(i - 1)

            body(0, ffn=False)
            pe.wait_ge(lo_done, NE)
            pe.wait_ge(wd_in, 16)
            with pe.Fori(1, NC - 1) as i:
                body(i)
            body(NC - 1, pre=False)
            for part in range(PARTS):
                for k in range(2 * BLOCKS):
                    (gate_up if k < BLOCKS else down)(NC - 1, part * BLOCKS + k % BLOCKS)
            ffn_tail(NC - 1)

        @block.scalar
        def _(act):
            def turned(c, k, which, dst, s_done):
                act.wait_ge(misc_filled, k + 1)
                b = c // CB
                nc.scalar.activation(dst[:].rearrange("p (q t) -> p t q", t=TB),
                                     misc[:].rearrange("p (t q) -> p t q", t=TB), ACT.Identity,
                                     scale=mod_sb[:, b, which + 1:which + 2],
                                     bias=mod_sb[:, b, which:which + 1]).then_inc(s_done, 1)
                act.wait_ge(s_done, c + 1)
                act.sem_inc(misc_drained, 1)

            def pre_h(c, k):
                turned(c, k, 0, h1, h1_ready)

            def post_h(c, k):
                if not is_first(c):
                    act.wait_ge(h2_ready, c)
                turned(c, k, 3, h2, h2_full)

            def take_xs(c, k, hf):
                act.wait_ge(misc_filled, k + 1)
                if not is_first(c):
                    act.wait_ge(conv_done, HALVES * c)
                nc.scalar.activation(xs_ext[:, hf, K - 1:], misc[:], ACT.Copy).then_inc(xs_ready, 1)
                act.wait_ge(xs_ready, HALVES * c + hf + 1)
                act.sem_inc(misc_drained, 1)

            def silu_xc(c, hf):
                act.wait_ge(conv_done, HALVES * c + hf + 1)
                nc.scalar.activation(xc[:, hf, :], xc[:, hf, :], ACT.Silu).then_inc(xc_ready, 1)

            def take_xdbl(c, k):
                act.wait_ge(misc_filled, k + 1)
                if not is_first(c):
                    act.wait_ge(bc_stored, 16 * c)
                nc.scalar.activation(x_dbl[0:R + 2 * N, :], misc[0:R + 2 * N, :], ACT.Copy).then_inc(xdbl_ready, 1)
                act.wait_ge(xdbl_ready, c + 1)
                act.sem_inc(misc_drained, 1)

            def take_z(c, k, hf):
                act.wait_ge(misc_filled, k + 1)
                bias = cols[:, hf, K + 1:K + 2]
                nc.scalar.activation(tok_z[:, hf, :], misc[:], ACT.Identity, bias=bias)
                if not is_first(c):
                    act.wait_ge(delta_ready, HALVES * c)
                nc.scalar.activation(log_part[:, hf, :], misc[:], ACT.Abs, bias=bias).then_inc(z_ready, 1)
                act.wait_ge(z_ready, HALVES * c + hf + 1)
                act.sem_inc(misc_drained, 1)

            def softplus(c):
                act.wait_ge(z_ready, HALVES * (c + 1))
                for hf in range(HALVES):
                    nc.scalar.activation(log_part[:, hf, :], log_part[:, hf, :], ACT.Exp, scale=-1.0).then_inc(sp_step, 1)
                for hf in range(HALVES):
                    act.wait_ge(sp_step, HALVES * c + hf + 1)
                    nc.scalar.activation(log_part[:, hf, :], log_part[:, hf, :], ACT.Ln, bias=1.0).then_inc(sp_ready, 1)

            def exps(c, j):
                for hf in range(HALVES):
                    u = HALVES * j + hf
                    act.wait_ge(delta_ready, HALVES * c + HALVES)
                    if is_first(c) and u < SLOTS:
                        act.wait_ge(lo_done, u + 1)
                    else:
                        act.wait_ge(unit_reduced, UNITS * c + u - SLOTS + 1)
                    for m in range(2):
                        n = 2 * j + m
                        last = nc.scalar.activation(ring[:, u % SLOTS, m, :], delta[:, hf, :], ACT.Exp,
                                                    scale=a_neg[:, hf, n:n + 1])
                    last.then_inc(exp_done, 1)

            def silu_gate(c, k, hf):
                act.wait_ge(misc_filled, k + 1)
                nc.scalar.activation(gate[:, hf, :], misc[:], ACT.Silu).then_inc(gate_ready, 1)
                act.wait_ge(gate_ready, HALVES * c + hf + 1)
                act.sem_inc(misc_drained, 1)

            def silu_g(c, b):
                act.wait_ge(g_ready, NB * c + b + 1)
                nc.scalar.activation(p_tile[:, b % BLOCKS, :], g_bank[b % 2][:], ACT.Silu).then_inc(silu_done, 1)

            def ffn_out(c):
                act.wait_ge(acc_ready, c + 1)
                nc.scalar.activation(f_t, acc[:], ACT.Identity, scale=mod_sb[:, c // CB, 5:6]).then_inc(ft_ready, 1)

            act.wait_ge(small_in, 16 * 8)
            nc.scalar.activation(sc[:], c_sb[:], ACT.Silu).then_inc(act_set, 1)
            nc.scalar.activation(a_neg[:], a_neg[:], ACT.Exp).then_inc(act_set, 1)
            act.wait_ge(act_set, 2)
            nc.scalar.activation(a_neg[:], a_neg[:], ACT.Copy, scale=-1.0).then_inc(act_set, 1)
            for e in range(NE):
                act.wait_ge(gu_in, 16 * (e + 1))
                nc.scalar.activation(gu_hi[:, e], ring[:, e], ACT.Copy).then_inc(hi_done, 1)
            act.wait_ge(dve_set, 10)
            act.wait_ge(act_set, 3)
            pre_h(0, 0)
            take_xs(0, 1, 0)
            take_xs(0, 2, 1)
            silu_xc(0, 0)
            silu_xc(0, 1)
            take_xdbl(0, 3)
            take_z(0, 4, 0)
            take_z(0, 5, 1)
            nc.scalar.preload_act_table_set(EXP_LN)
            softplus(0)
            exps(0, 0)
            exps(0, 1)

            def body(i, pre=True, ffn=True):
                for part in range(PARTS):
                    if part < 3 or pre:
                        nc.scalar.preload_act_table_set(EXP_LN)
                    if part < 3:
                        exps(i, 2 * part + 2)
                        exps(i, 2 * part + 3)
                        if part == 2 and pre:
                            softplus(i + 1)
                    elif pre:
                        exps(i + 1, 0)
                        exps(i + 1, 1)
                    nc.scalar.preload_act_table(ACT.Silu)
                    behind = {}
                    if part == 0:
                        behind[-1] = lambda: silu_gate(i, misc_post(i, 0), 0)
                        behind[0] = lambda: silu_gate(i, misc_post(i, 1), 1)
                        if pre:
                            behind[2] = lambda: pre_h(i + 1, misc_pre(i, 0))
                            behind[4] = lambda: take_xs(i + 1, misc_pre(i, 1), 0)
                            behind[6] = lambda: take_xs(i + 1, misc_pre(i, 2), 1)
                    if part == 1 and pre:
                        silu_xc(i + 1, 0)
                        silu_xc(i + 1, 1)
                        behind[3] = lambda: take_xdbl(i + 1, misc_pre(i, 3))
                        behind[6] = lambda: take_z(i + 1, misc_pre(i, 4), 0)
                        behind[7] = lambda: take_z(i + 1, misc_pre(i, 5), 1)
                    for k in range(-1, BLOCKS):
                        if ffn and k >= 0:
                            silu_g(i - 1, part * BLOCKS + k)
                        if k in behind:
                            behind[k]()
                    if part == 3:
                        post_h(i, misc_post(i, 3))
                        if ffn:
                            ffn_out(i - 1)

            body(0, ffn=False)
            with act.Fori(1, NC - 1) as i:
                body(i)
            body(NC - 1, pre=False)
            for b in range(NB):
                silu_g(NC - 1, b)
            ffn_out(NC - 1)

        @block.vector
        def _(dve):
            def norm_stats(which, c, src):
                step, base = ln_step[which], 4 * c
                stats, mv = ln_in[:, which], ln_mv[:, which]
                for t in range(TB):
                    last = nc.vector.bn_stats(stats[:, t, :], src(t))
                last.then_inc(step, 1)
                dve.wait_ge(step, base + 1)
                dve.sem_inc(step, 1)
                for t in range(TB):
                    last = nc.vector.bn_aggr(mv[:, t, :], stats[:, t, :])
                last.then_inc(step, 1)
                dve.wait_ge(step, base + 3)
                nc.vector.tensor_scalar(ln_ve[:, which, :], mv[:, :, 1], EPS, None, ALU.add).then_inc(step, 1)

            def norm_apply(which, c, src, dst):
                dve.wait_ge(ln_ready[which], c + 1)
                for t in range(TB):
                    last = nc.vector.tensor_scalar(dst(t), src(t), ln_mv[:, which, t, 0:1],
                                                   ln_rstd[:, which, t:t + 1], ALU.subtract, ALU.mult)
                last.then_inc(xn_ready[which], 1)

            def pre_stats(c):
                dve.wait_ge(x_loaded, 16 * (c + 1))
                norm_stats(0, c, lambda t: tok[:, t, :])

            def pre_apply(c):
                norm_apply(0, c, lambda t: tok[:, t, :], lambda t: tok[:, t, :])

            def conv(c, hf):
                n_step, n_halo = (K - 1) * (HALVES * c + hf), 2 * (HALVES * c + hf)
                nc.vector.tensor_copy(xs_ext[:, hf, 0:K - 1], halo[:, c % CB, hf, :]).then_inc(halo_in, 1)
                dve.wait_ge(halo_in, n_halo + 1)
                dve.wait_ge(xs_ready, HALVES * c + hf + 1)
                nc.vector.tensor_copy(halo[:, c % CB + 1, hf, :], xs_ext[:, hf, L:]).then_inc(halo_in, 1)
                nc.vector.tensor_scalar(xc[:, hf, :], xs_ext[:, hf, K - 1:], cols[:, hf, K - 1:K], cols[:, hf, K:K + 1],
                                        ALU.mult, ALU.add).then_inc(conv_step, 1)
                for k in range(K - 1):
                    dve.wait_ge(conv_step, n_step + k + 1)
                    nc.vector.scalar_tensor_tensor(out=xc[:, hf, :], in0=xs_ext[:, hf, k:k + L],
                                                   scalar=cols[:, hf, k:k + 1], in1=xc[:, hf, :], op0=ALU.mult,
                                                   op1=ALU.add).then_inc(conv_step if k < K - 2 else conv_done, 1)
                dve.wait_ge(halo_in, n_halo + 2)
                dve.wait_ge(conv_done, HALVES * c + hf + 1)

            def finish_delta(c, hf):
                if hf == 0 and not is_first(c):
                    dve.wait_ge(exp_done, UNITS * c)
                dve.wait_ge(sp_ready, HALVES * c + hf + 1)
                nc.vector.scalar_tensor_tensor(out=delta[:, hf, :], in0=tok_z[:, hf, :], scalar=0.0,
                                               in1=log_part[:, hf, :], op0=ALU.max,
                                               op1=ALU.add).then_inc(delta_ready, 1)

            def take_du(c, hf):
                dve.wait_ge(delta_ready, HALVES * c + hf + 1)
                nc.vector.tensor_tensor(du[:, hf, :], delta[:, hf, :], xc[:, hf, :], ALU.mult).then_inc(du_ready, 1)

            def dbu(c, j, hf, m):
                if m == 0:
                    dve.wait_ge(b_loaded[j % 2], 16 * (PAIRS // 2 * c + j // 2 + 1))
                    dve.wait_ge(du_ready, HALVES * c + HALVES)
                if not (is_first(c) and j == 0 and hf == 0):
                    dve.wait_ge(scan_step, 2 * N * c + 2 * (HALVES * j + hf) + m - 1)
                nc.vector.tensor_tensor(dbu_bank[m][:], du[:, hf, :], b_tile[:, j % 2, m, :],
                                        ALU.mult).then_inc(dbu_done, 1)

            def scan(c, j, hf, m):
                u = HALVES * j + hf
                if m == 0:
                    dve.wait_ge(exp_done, UNITS * c + u + 1)
                dve.wait_ge(dbu_done, 2 * N * c + 2 * u + m + 1)
                n = 2 * j + m
                h = ring[:, u % SLOTS, m, :]
                nc.vector.tensor_tensor_scan(h, h, dbu_bank[m][:], carry[:, c % CB, hf, n:n + 1], ALU.mult,
                                             ALU.add).then_inc(scan_step, 1)

            def keep_carry(c, j, hf):
                u = HALVES * j + hf
                dve.wait_ge(scan_step, 2 * N * c + 2 * u + 2)
                nc.vector.tensor_copy(carry[:, c % CB + 1, hf, 2 * j:2 * j + 2],
                                      ring[:, u % SLOTS, :, L - 1]).then_inc(scan_done, 1)

            def times_u(c, b):
                dve.wait_ge(silu_done, NB * c + b + 1)
                dve.wait_ge(u_ready, NB * c + b + 1)
                p = p_tile[:, b % BLOCKS, :]
                nc.vector.tensor_tensor(p, u_bank[b % 2][:], p, ALU.mult).then_inc(p_ready, 1)

            def gated(c):
                dve.wait_ge(gate_ready, HALVES * (c + 1))
                dve.wait_ge(unit_reduced, UNITS * (c + 1))
                for hf in range(HALVES):
                    nc.vector.tensor_tensor(gate[:, hf, :], gate[:, hf, :], y[:, hf, :], ALU.mult).then_inc(r_ready, 1)

            def residual(c, k):
                dve.wait_ge(misc_filled, k + 1)
                dve.wait_ge(xres_loaded, 16 * (c + 1))
                t = x1[:, c % 2].rearrange("p t h -> p (t h)")
                nc.vector.tensor_tensor(t, misc[:], t, ALU.add).then_inc(x1_ready, 1)
                dve.wait_ge(x1_ready, c + 1)
                dve.sem_inc(misc_drained, 1)

            def post_stats(c):
                norm_stats(1, c, lambda t: x1[:, c % 2, t, :])

            def post_apply(c):
                norm_apply(1, c, lambda t: x1[:, c % 2, t, :], lambda t: tok2[:, t, :])

            def split_h2(c):
                dve.wait_ge(h2_full, c + 1)
                nc.vector.tensor_copy(h2_hi[:], h2[:]).then_inc(h2_step, 1)
                dve.wait_ge(h2_step, c + 1)
                nc.vector.tensor_tensor(h2_lo[:], h2[:], h2_hi[:].bitcast(F32), ALU.subtract).then_inc(h2_ready, 1)

            def add_ffn(c):
                dve.wait_ge(ft_turned, c + 1)
                t = x1[:, c % 2].rearrange("p t h -> p (t h)")
                nc.vector.tensor_tensor(t, acc[:], t, ALU.add).then_inc(out_ready, 1)

            nc.vector.memset(halo[:], 0.0).then_inc(dve_set, 1)
            nc.vector.memset(carry[:], 0.0).then_inc(dve_set, 1)
            nc.vector.memset(sc_wide, 1.0).then_inc(dve_set, 1)
            dve.wait_ge(act_set, 1)
            dve.wait_ge(dve_set, 3)
            for b in range(B):
                last = nc.vector.tensor_scalar(sc_wide[:, b, :], sc_wide[:, b, :], sc[:, b:b + 1], None, ALU.mult)
            last.then_inc(dve_set, 1)
            pre_stats(0)
            pre_apply(0)
            dve.wait_ge(pe_set, 1)
            nc.vector.tensor_copy(mod_sb[:], acc[:, 0:6 * B].rearrange("p (k b) -> p b k", b=B)).then_inc(dve_set, 1)
            dve.wait_ge(dve_set, 5)
            for k in (1, 4):
                last = nc.vector.tensor_scalar(mod_sb[:, :, k], mod_sb[:, :, k], 1.0, None, ALU.add)
            last.then_inc(dve_set, 1)

            def clamp(v, sign, count):
                nc.vector.tensor_scalar(sign, v, 0.0, 2.0, ALU.is_ge, ALU.mult).then_inc(dve_set, 1)
                dve.wait_ge(dve_set, count + 1)
                nc.vector.tensor_scalar(sign, sign, -1.0, None, ALU.add).then_inc(dve_set, 1)
                dve.wait_ge(dve_set, count + 2)
                nc.vector.tensor_tensor(v, v, sign, ALU.mult).then_inc(dve_set, 1)
                dve.wait_ge(dve_set, count + 3)
                nc.vector.scalar_tensor_tensor(out=v, in0=v, scalar=0.25, in1=sign, op0=ALU.max,
                                               op1=ALU.mult).then_inc(dve_set, 1)
                dve.wait_ge(dve_set, count + 4)

            clamp(mod_sb[:, :, 5], gb_sign[:], 6)
            dve.wait_ge(pe_set, 2)
            nc.vector.tensor_copy(ga_row, u_bank[0][:, 0:B * H].rearrange("p (b h) -> p b h", b=B)).then_inc(dve_set, 1)
            dve.wait_ge(dve_set, 11)
            clamp(ga_row, ga_sign, 11)
            for b in range(B):
                for hf in range(HALVES):
                    last = nc.vector.tensor_tensor(w_out_ga[:, b, hf, :], w_out_sb[:, hf, :], ga_row[:, b, :], ALU.mult)
            last.then_inc(dve_set, 1)
            dve.wait_ge(dve_set, 16)
            conv(0, 0)
            conv(0, 1)
            for hf in range(HALVES):
                finish_delta(0, hf)
                take_du(0, hf)

            late = []

            def unit(c, j, hf, mults):
                def mult():
                    if mults:
                        mults.pop(0)()
                dbu(c, j, hf, 0)
                keep_late()
                mult()
                dbu(c, j, hf, 1)
                mult()
                scan(c, j, hf, 0)
                mult()
                scan(c, j, hf, 1)
                mult()
                late.append((c, j, hf))

            def keep_late():
                if late:
                    keep_carry(*late.pop())

            for j in range(2):
                for hf in range(HALVES):
                    unit(0, j, hf, [])
            keep_late()

            def body(i, pre=True, ffn=True):
                def mults(part, first, n):
                    return [lambda b=b: times_u(i - 1, b)
                            for b in range(part * BLOCKS + first, part * BLOCKS + first + n)] if ffn else []

                for part in range(PARTS - 1):
                    j = 2 * part + 2
                    if part == 0 and pre:
                        pre_stats(i + 1)
                    if part == 1 and pre:
                        conv(i + 1, 1)
                    unit(i, j, 0, [])
                    if part == 0 and pre:
                        keep_late()
                        pre_apply(i + 1)
                    unit(i, j, 1, [])
                    keep_late()
                    if part == 2 and pre:
                        finish_delta(i + 1, 0)
                        finish_delta(i + 1, 1)
                    unit(i, j + 1, 0, mults(part, 0, 4))
                    unit(i, j + 1, 1, mults(part, 4, 4))
                    keep_late()
                    if part == 0 and pre:
                        conv(i + 1, 0)
                if pre:
                    take_du(i + 1, 0)
                    take_du(i + 1, 1)
                    dve.wait_ge(scan_done, UNITS * (i + 1))
                    unit(i + 1, 0, 0, [])
                    unit(i + 1, 0, 1, [])
                    unit(i + 1, 1, 0, mults(3, 0, 4))
                    keep_late()
                else:
                    for mult in mults(3, 0, 4):
                        mult()
                gated(i)
                for mult in mults(3, 4, 2):
                    mult()
                residual(i, misc_post(i, 2))
                post_stats(i)
                for mult in mults(3, 6, 2):
                    mult()
                if pre:
                    unit(i + 1, 1, 1, [lambda: post_apply(i)])
                    keep_late()
                else:
                    post_apply(i)
                split_h2(i)
                if ffn:
                    add_ffn(i - 1)

            body(0, ffn=False)
            with dve.Fori(1, NC - 1) as i:
                body(i)
            body(NC - 1, pre=False)
            for b in range(NB):
                times_u(NC - 1, b)
            add_ffn(NC - 1)

        @block.gpsimd
        def _(pool):
            def rstd(which, c):
                pool.wait_ge(ln_step[which], 4 * (c + 1))
                nc.gpsimd.tensor_tensor(ln_rstd[:, which, :], ln_ve[:, which, :], minus_half[:],
                                        ALU.pow).then_inc(ln_ready[which], 1)

            def reduce_unit(c, j, hf):
                u = HALVES * j + hf
                step = 2 * (UNITS * c + u)
                pool.wait_ge(scan_done, UNITS * c + u + 1)
                if hf == 0:
                    pool.wait_ge(c_loaded[j % 4], 16 * (PAIRS // 4 * c + j // 4 + 1))
                hc = ring[:, u % SLOTS]
                nc.gpsimd.tensor_tensor(hc, hc, c_tile[:, j % 4], ALU.mult).then_inc(pool_step, 1)
                pool.wait_ge(pool_step, step + 1)
                nc.gpsimd.tensor_tensor(hc[:, 0, :], hc[:, 0, :], hc[:, 1, :], ALU.add).then_inc(pool_step, 1)
                if j == 0:
                    return
                pool.wait_ge(pool_step, step + 2)
                if j == 1:
                    if hf == 0 and not is_first(c):
                        pool.wait_ge(r_ready, HALVES * c)
                    so_far = ring[:, (u - HALVES) % SLOTS, 0, :]
                else:
                    pool.wait_ge(unit_reduced, UNITS * c + u - 1)
                    so_far = y[:, hf, :]
                nc.gpsimd.tensor_tensor(y[:, hf, :], so_far, hc[:, 0, :], ALU.add).then_inc(unit_reduced, 1)
                if (j, hf) == (1, 1):
                    pool.wait_ge(unit_reduced, UNITS * c + 2)
                    pool.sem_inc(unit_reduced, 2)

            nc.gpsimd.memset(minus_half[:], -0.5).then_inc(pool_set, 1)
            nc.gpsimd.memset(ident[:], 0.0).then_inc(pool_set, 1)
            pool.wait_ge(pool_set, 2)
            nc.gpsimd.affine_select(out=ident[:], in_=ident[:], compare_op=ALU.not_equal, fill=1.0, base=0,
                                    pattern=[[-1, P]], channel_multiplier=1).then_inc(pool_set, 1)
            rstd(0, 0)
            for e in range(NE):
                pool.wait_ge(hi_done, e + 1)
                nc.gpsimd.tensor_tensor(gu_lo[:, e], ring[:, e], gu_hi[:, e].bitcast(F32),
                                        ALU.subtract).then_inc(lo_done, 1)
            for j in range(2):
                for hf in range(HALVES):
                    reduce_unit(0, j, hf)

            def body(i, pre=True):
                if pre:
                    rstd(0, i + 1)
                for part in range(PARTS):
                    c, j = (i, 2 * part + 2) if part < 3 else (i + 1, 0)
                    if part < 3 or pre:
                        reduce_unit(c, j, 0)
                        reduce_unit(c, j, 1)
                        reduce_unit(c, j + 1, 0)
                    if part == 3:
                        rstd(1, i)
                    if part < 3 or pre:
                        reduce_unit(c, j + 1, 1)

            with pool.Fori(0, NC - 1) as i:
                body(i)
            body(NC - 1, pre=False)


def kernel(**inputs):
    import numpy as np
    import concourse.bacc as bacc
    from concourse.bass_utils import run_bass_kernel_spmd

    a = {k: np.asarray(v) for k, v in inputs.items()}

    def halves(t):
        return t.reshape(HALVES, P, -1).transpose(1, 0, 2)

    cols = np.concatenate([halves(a["L0_attn_conv_w"].reshape(D, K)), halves(a["L0_attn_conv_b"].reshape(D, 1)),
                           halves(a["L0_attn_b_dt"].reshape(D, 1))], axis=2)
    gu = np.stack([a["L0_ffn_Wg"], a["L0_ffn_Wu"]], axis=2)
    arrays = {
        "x": a["L0_attn_x"].reshape(NC * P, TB * H),
        "w_in": a["L0_attn_W_in"].T,
        "cols": cols,
        "w_x": halves(a["L0_attn_W_x"].T),
        "w_dt": a["L0_attn_W_dt"].T,
        "a_log": halves(a["L0_attn_A_log"]),
        "w_out": halves(a["L0_attn_W_out"].T),
        "w_gu": gu.transpose(1, 0, 2, 3),
        "w_d": a["L0_ffn_Wd"].reshape(NB, P, H).transpose(1, 0, 2),
        "c_t": a["L0_c"].T,
        "w_mod": a["L0_wmod"],
    }
    arrays = {k: np.ascontiguousarray(v) for k, v in arrays.items()}
    nc = bacc.Bacc("TRN2", target_bir_lowering=False, num_devices=1)
    t = {k: nc.dram_tensor("in_" + k, v.shape, F32, kind="ExternalInput").ap() for k, v in arrays.items()}
    out = nc.dram_tensor("out_tokens", (NC * P, TB * H), F32, kind="ExternalOutput").ap()
    bc_dram = nc.dram_tensor("bc_rows", (NC * 2 * N, L), F32, kind="Internal").ap()
    build(nc, t["x"], t["w_in"], t["cols"], t["w_x"], t["w_dt"], t["a_log"], t["w_out"], t["w_gu"],
          t["w_d"], t["c_t"], t["w_mod"], out, bc_dram)
    r = run_bass_kernel_spmd(nc, [{"in_" + k: v for k, v in arrays.items()}], core_ids=[0])
    return r.results[0]["out_tokens"].reshape(B, S, H)
```

```python
from contextlib import ExitStack

import concourse.bass as bass
from concourse import mybir

F32 = mybir.dt.float32
F32R = mybir.dt.float32r
ALU = mybir.AluOpType
ACT = mybir.ActivationFunctionType

P = 128
B, S, H = 2, 2048, 128
D, N, R, K = 256, 16, 64, 4
NE, F = 8, 512
L = 512
NC = B * S // L
CB = S // L
HALVES = D // P
PAIRS = N // 2
UNITS = PAIRS * HALVES
TB = L // P
FB = F // P
NB = NE * FB
PARTS = 4
BLOCKS = NB // PARTS
SLOTS = 8
HC_DVE = 15
EPS = 1e-5
EXP_LN = "natural_log_exp_and_others"
MISC_PRE, MISC_POST = 6, 4
MISC = MISC_PRE + MISC_POST


def is_first(c):
    return isinstance(c, int) and c == 0


def build(nc, x, w_in, cols_in, w_x, w_dt, a_log, w_out, w_gu, w_d, c_t, w_mod, out, bc_dram):
    with ExitStack() as ctx:
        def sb(name, shape, dt=F32):
            return ctx.enter_context(nc.sbuf_tensor(name, shape, dt))

        def bank(name):
            return ctx.enter_context(nc.psum_tensor(name, [P, 512], F32))

        def sem(name):
            return ctx.enter_context(nc.semaphore(name))

        gu_hi = sb("gu_hi", [P, NE, 2, F], F32R)
        gu_lo = sb("gu_lo", [P, NE, 2, F], F32R)
        wd = sb("wd", [P, NB, H])
        w_in_sb = sb("w_in_sb", [P, 2 * D])
        w_x_sb = sb("w_x_sb", [P, HALVES, R + 2 * N])
        w_dt_sb = sb("w_dt_sb", [R, D])
        w_out_ga = sb("w_out_ga", [P, B, HALVES, H])
        cols = sb("cols", [P, HALVES, K + 2])
        a_neg = sb("a_neg", [P, HALVES, N])
        ident = sb("ident", [P, P])
        c_sb = sb("c_sb", [P, B])
        sc = sb("sc", [P, B])
        mod_sb = sb("mod_sb", [P, B, 6])
        gb_sign = sb("gb_sign", [P, B])
        minus_half = sb("minus_half", [P, TB])
        tok_z = sb("tok_z", [P, 2, L])
        tok, tok2 = (tok_z[:, k].rearrange("p (t h) -> p t h", t=TB) for k in range(2))
        ln_in = sb("ln_in", [P, 2, TB, 6])
        ln_mv = sb("ln_mv", [P, 2, TB, 2])
        ln_ve = sb("ln_ve", [P, 2, TB])
        ln_rstd = sb("ln_rstd", [P, 2, TB])
        minus_mean = sb("minus_mean", [P, TB])
        h1 = sb("h1", [P, L])
        xs_ext = sb("xs_ext", [P, HALVES, K - 1 + L])
        halo = sb("halo", [P, CB + 1, HALVES, K - 1])
        x_dbl = sb("x_dbl", [P, L])
        b_tile = sb("b_tile", [P, 2, 2, L])
        carry = sb("carry", [P, CB + 1, HALVES, N])
        y = sb("y", [P, HALVES, L])
        gate = sb("gate", [P, HALVES, L])
        x1 = sb("x1", [P, 2, TB, H])
        h2 = sb("h2", [P, L])
        h2_hi = sb("h2_hi", [P, L], F32R)
        h2_lo = sb("h2_lo", [P, L], F32R)
        p_tile = sb("p_tile", [P, BLOCKS, L])
        sc_wide, ga_row, ga_sign, w_out_sb = (p_tile[:, k, 0:2 * P].rearrange("p (b h) -> p b h", b=2) for k in range(4))
        f_t = xs_ext[:, 0, 0:L]

        with ExitStack() as until_last:
            def sb_until_last(name, shape):
                return until_last.enter_context(nc.sbuf_tensor(name, shape, F32))

            ring = sb_until_last("ring", [P, SLOTS, 2, L])
            c_tile = sb_until_last("c_tile", [P, 4, 2, L])
            xc = sb_until_last("xc", [P, HALVES, L])
            log_part = sb_until_last("log_part", [P, HALVES, L])
            delta = sb_until_last("delta", [P, HALVES, L])
            du = sb_until_last("du", [P, HALVES, L])
        wd_hi, wd_lo = sb("wd_hi", [P, NB, H], F32R), sb("wd_lo", [P, NB, H], F32R)
        p_hi, p_lo = sb("p_hi", [P, BLOCKS, L], F32R), sb("p_lo", [P, BLOCKS, L], F32R)

        g_bank = [bank("g0"), bank("g1")]
        u_bank = [bank("u0"), bank("u1")]
        acc = bank("acc")
        dbu_bank = [bank("dbu0"), bank("dbu1")]
        misc = bank("misc")

        mod_in, small_in, wd_in = sem("mod_in"), sem("small_in"), sem("wd_in")
        gu_in = [sem(f"gu_in{k}") for k in range(NE // 2)]
        dve_set, act_set, pe_set, pool_set = sem("dve_set"), sem("act_set"), sem("pe_set"), sem("pool_set")
        hi_done, lo_done = sem("hi_done"), sem("lo_done")
        x_loaded, xres_loaded, out_stored, bc_stored = (
            sem("x_loaded"), sem("xres_loaded"), sem("out_stored"), sem("bc_stored"))
        b_loaded = [sem(f"b_loaded{i}") for i in range(2)]
        c_loaded = [sem(f"c_loaded{i}") for i in range(4)]
        bc_seen = sem("bc_seen")
        misc_filled, misc_drained = sem("misc_filled"), sem("misc_drained")
        hc_given = sem("hc_given")
        hc_ready = sem("hc_ready")
        ln_step = [sem("ln1_step"), sem("ln2_step")]
        ln1_rstd = sem("ln1_rstd")
        ln_ready = [sem("ln1_ready"), sem("ln2_ready")]
        xn_ready = [sem("xn1_ready"), sem("xn2_ready")]
        h1_ready, xs_ready, halo_in, conv_step, conv_done, xc_ready = (
            sem("h1_ready"), sem("xs_ready"), sem("halo_in"), sem("conv_step"), sem("conv_done"), sem("xc_ready"))
        xdbl_ready, z_ready, sp_step, sp_ready, delta_ready, du_ready = (
            sem("xdbl_ready"), sem("z_ready"), sem("sp_step"), sem("sp_ready"), sem("delta_ready"), sem("du_ready"))
        exp_done, dbu_done, scan_step, scan_done, pool_step, unit_reduced = (
            sem("exp_done"), sem("dbu_done"), sem("scan_step"), sem("scan_done"), sem("pool_step"), sem("unit_reduced"))
        gate_ready, r_ready, x1_ready, h2_full, h2_step, h2_ready = (
            sem("gate_ready"), sem("r_ready"), sem("x1_ready"), sem("h2_full"), sem("h2_step"), sem("h2_ready"))
        g_ready, u_ready, silu_done, p_ready, acc_ready, ft_ready, ft_turned, out_ready = (
            sem("g_ready"), sem("u_ready"), sem("silu_done"), sem("p_ready"), sem("acc_ready"), sem("ft_ready"),
            sem("ft_turned"), sem("out_ready"))

        def chunk_rows(t, c):
            return t[bass.ts(c, P), :]

        def misc_pre(i, k):
            return k if isinstance(i, int) and i < 0 else MISC_PRE + MISC * i + 2 + k

        def second_bank(c, hf):
            return u_bank[1] if isinstance(c, int) and c <= 1 and hf == 1 else misc

        def misc_post(i, k):
            last = 0 if isinstance(i, int) and i == NC - 1 else MISC_PRE
            return MISC_PRE + MISC * i + k + (last if k >= 2 else 0)

        wd_hi_done, wd_lo_done, p_hi_ready, p_lo_ready = (
            sem("wd_hi_done"), sem("wd_lo_done"), sem("p_hi_ready"), sem("p_lo_ready"))

        block = ctx.enter_context(nc.Block())

        @block.sync
        def _(sp):
            def load_x(c):
                if not is_first(c):
                    sp.wait_ge(delta_ready, HALVES * c)
                sp.dma_start(tok_z[:, 0], chunk_rows(x, c)).then_inc(x_loaded, 16)

            def load_residual(c, stored):
                if stored is not None:
                    sp.wait_ge(out_stored, stored)
                sp.dma_start(x1[:, c % 2].rearrange("p t h -> p (t h)"), chunk_rows(x, c)).then_inc(xres_loaded, 16)

            def store_bc(c):
                sp.wait_ge(xdbl_ready, c + 1)
                sp.dma_start(bc_dram[bass.ts(c, 2 * N), :], x_dbl[R:R + 2 * N, :]).then_inc(bc_stored, 16)

            def load_pair(c, j):
                if j == 0:
                    sp.wait_ge(bc_stored, 16 * (c + 1))
                    sp.sem_inc(bc_seen, 1)
                def rows(first):
                    return bc_dram[bass.ds(2 * N * c + first + 2 * j, 2), :].partition_broadcast(P)
                if not (is_first(c) and j < 2):
                    sp.wait_ge(dbu_done, 2 * N * c + 4 * (j - 1))
                sp.dma_start(b_tile[:, j % 2], rows(0)).then_inc(b_loaded[j % 2], 16)
                if not (is_first(c) and j < 4):
                    sp.wait_ge(unit_reduced, UNITS * c + 2 * (j - 3))
                sp.dma_start(c_tile[:, j % 4], rows(N)).then_inc(c_loaded[j % 4], 16)

            def store_out(c):
                sp.wait_ge(out_ready, c + 1)
                sp.dma_start(chunk_rows(out, c), x1[:, c % 2].rearrange("p t h -> p (t h)")).then_inc(out_stored, 16)

            load_x(0)
            sp.dma_start(c_sb[:], c_t).then_inc(mod_in, 16)
            sp.dma_start(b_tile[:].rearrange("p a b l -> p (a b l)")[:, 0:6 * H], w_mod).then_inc(mod_in, 16)
            for dst, src in ((w_in_sb, w_in), (cols, cols_in), (w_x_sb, w_x), (w_dt_sb, w_dt), (a_neg, a_log)):
                sp.dma_start(dst[:], src).then_inc(small_in, 16)
            sp.dma_start(w_out_sb, w_out).then_inc(small_in, 16)
            for k in range(NE // 2):
                sp.dma_start(ring[:, 2 * k:2 * k + 2], w_gu[:, 2 * k:2 * k + 2]).then_inc(gu_in[k], 16)
            load_residual(0, None)
            sp.dma_start(wd[:], w_d).then_inc(wd_in, 16)
            store_bc(0)
            sp.wait_ge(pe_set, 2)
            load_pair(0, 0)
            load_pair(0, 1)

            def body(i, pre=True, late=True):
                if pre:
                    load_x(i + 1)
                load_pair(i, 2)
                load_pair(i, 3)
                if late:
                    store_out(i - 2)
                    load_residual(i, 16 * (i - 1))
                load_pair(i, 4)
                load_pair(i, 5)
                load_pair(i, 6)
                load_pair(i, 7)
                if pre:
                    store_bc(i + 1)
                    load_pair(i + 1, 0)
                    load_pair(i + 1, 1)

            body(0, late=False)
            load_residual(1, None)
            body(1, late=False)
            with sp.Fori(2, NC - 1) as i:
                body(i)
            body(NC - 1, pre=False)
            store_out(NC - 2)
            store_out(NC - 1)
            sp.wait_ge(out_stored, 16 * NC)
            sp.wait_ge(bc_stored, 16 * NC)

        @block.tensor
        def _(pe):
            def add_unit(u):
                pe.wait_ge(hc_ready, u + 1)
                for m in range(2):
                    last = nc.tensor.matmul(g_bank[u % HALVES][:], ident[:], ring[:, u % SLOTS, m, :],
                                            start=(u < HALVES and m == 0), stop=(u >= UNITS - HALVES and m == 1))
                last.then_inc(unit_reduced, 1)

            def use_misc(k):
                if not is_first(k):
                    pe.wait_ge(misc_drained, k)

            def turn(dst, src, s_done):
                for t in range(TB):
                    last = nc.tensor.transpose(dst(t), src(t), ident[:])
                last.then_inc(s_done, 1)

            def pre_turn(c, k):
                use_misc(k)
                pe.wait_ge(xn_ready[0], c + 1)
                turn(lambda t: misc[:, t * P:(t + 1) * P], lambda t: tok[:, t, :], misc_filled)

            def in_proj(c, k, block_):
                to = misc if block_ >= HALVES and not is_first(c) else second_bank(c, block_ % HALVES)
                if to is misc:
                    use_misc(k)
                pe.wait_ge(h1_ready, c + 1)
                nc.tensor.matmul(to[:], w_in_sb[:, block_ * P:(block_ + 1) * P], h1[:], start=True,
                                 stop=True).then_inc(misc_filled, 1)

            def x_proj(c, k):
                use_misc(k)
                pe.wait_ge(xc_ready, 2 * c + 2)
                for hf in range(HALVES):
                    last = nc.tensor.matmul(misc[0:R + 2 * N, :], w_x_sb[:, hf, :], xc[:, hf, :],
                                            start=(hf == 0), stop=(hf == 1))
                last.then_inc(misc_filled, 1)

            def dt_proj(c, k, hf):
                to = second_bank(c, hf)
                if to is misc:
                    use_misc(k)
                pe.wait_ge(xdbl_ready, c + 1)
                nc.tensor.matmul(to[:], w_dt_sb[:, hf * P:(hf + 1) * P], x_dbl[0:R, :], start=True,
                                 stop=True).then_inc(misc_filled, 1)

            def out_proj(c, k):
                use_misc(k)
                pe.wait_ge(r_ready, 2 * c + 2)
                for t in range(TB):
                    for hf in range(HALVES):
                        r_t = gate[:, hf, :].rearrange("p (q t) -> p t q", t=TB)[:, t, :]
                        last = nc.tensor.matmul(misc[:, t * P:(t + 1) * P], r_t, w_out_ga[:, c // CB, hf, :],
                                                start=(hf == 0), stop=(hf == 1))
                last.then_inc(misc_filled, 1)

            def post_turn(c, k):
                use_misc(k)
                pe.wait_ge(xn_ready[1], c + 1)
                turn(lambda t: misc[:, t * P:(t + 1) * P], lambda t: tok2[:, t, :], misc_filled)

            def gate_up(c, b):
                e, f = b // FB, (b % FB) * P
                if b == 0:
                    pe.wait_ge(h2_ready, c + 1)
                for which, to, used, s_done in ((0, g_bank, silu_done, g_ready), (1, u_bank, p_ready, u_ready)):
                    if b % BLOCKS >= 2:
                        pe.wait_ge(used, NB * c + b - 1)
                    w_hi, w_lo = gu_hi[:, e, which, f:f + P], gu_lo[:, e, which, f:f + P]
                    nc.tensor.matmul(to[b % 2][:], w_hi, h2_hi[:], start=True, stop=False)
                    nc.tensor.matmul(to[b % 2][:], w_hi, h2_lo[:], start=False, stop=False)
                    nc.tensor.matmul(to[b % 2][:], w_lo, h2_hi[:], start=False, stop=True).then_inc(s_done, 1)

            def down(c, b):
                pe.wait_ge(p_ready, NB * c + b + 1)
                last = nc.tensor.matmul(acc[:], wd[:, b, :], p_tile[:, b % BLOCKS, :], start=(b == 0),
                                        stop=(b == NB - 1))
                if b == NB - 1:
                    last.then_inc(acc_ready, 1)

            def down_split(b):
                pe.wait_ge(p_lo_ready, b + 1)
                w_hi, w_lo = wd_hi[:, b, :], wd_lo[:, b, :]
                nc.tensor.matmul(acc[:], w_hi, p_hi[:, b % BLOCKS, :], start=(b == 0), stop=False)
                nc.tensor.matmul(acc[:], w_lo, p_hi[:, b % BLOCKS, :], start=False, stop=False)
                last = nc.tensor.matmul(acc[:], w_hi, p_lo[:, b % BLOCKS, :], start=False, stop=(b == NB - 1))
                if b == NB - 1:
                    last.then_inc(acc_ready, 1)

            def ffn_tail(c):
                pe.wait_ge(ft_ready, c + 1)
                turn(lambda t: acc[:, t * P:(t + 1) * P],
                     lambda t: f_t.rearrange("p (q t) -> p t q", t=TB)[:, t, :], ft_turned)

            pe.wait_ge(mod_in, 16 * 2)
            pe.wait_ge(act_set, 1)
            w_mod_sb = b_tile[:].rearrange("p a b l -> p (a b l)")[:, 0:6 * H]
            for k in range(6):
                last = nc.tensor.matmul(acc[:, B * k:B * k + B], w_mod_sb[:, k * H:(k + 1) * H], sc[:], start=True,
                                        stop=True)
            last.then_inc(pe_set, 1)
            pe.wait_ge(pool_set, 3)
            pre_turn(0, 0)
            pe.wait_ge(dve_set, 4)
            for b in range(B):
                last = nc.tensor.matmul(u_bank[0][:, b * H:(b + 1) * H], sc_wide[:, b, :],
                                        w_mod_sb[:, 2 * H:3 * H], start=True, stop=True)
            last.then_inc(pe_set, 1)
            pe.wait_ge(small_in, 16 * 6)
            in_proj(0, 1, 0)
            in_proj(0, 2, 1)
            x_proj(0, 3)
            dt_proj(0, 4, 0)
            dt_proj(0, 5, 1)
            def body(i, pre=True, tail=True):
                tasks = {}
                if tail:
                    tasks[0, 1] = lambda: ffn_tail(i - 2)
                tasks[0, -1] = lambda: in_proj(i, misc_post(i, 0), 2)
                tasks[0, 2] = lambda: in_proj(i, misc_post(i, 1), 3)
                if pre:
                    tasks[0, 5] = lambda: pre_turn(i + 1, misc_pre(i, 0))
                    tasks[0, 7] = lambda: in_proj(i + 1, misc_pre(i, 1), 0)
                    tasks[0, 8] = lambda: in_proj(i + 1, misc_pre(i, 2), 1)
                    tasks[1, 2] = lambda: x_proj(i + 1, misc_pre(i, 3))
                    tasks[1, 4] = lambda: dt_proj(i + 1, misc_pre(i, 4), 0)
                    tasks[1, 8] = lambda: dt_proj(i + 1, misc_pre(i, 5), 1)
                tasks[3, 7] = lambda: out_proj(i, misc_post(i, 2))
                tasks[3, 14] = lambda: post_turn(i, misc_post(i, 3))
                for part in range(PARTS):
                    for k in range(-1, 2 * BLOCKS):
                        if k >= 0:
                            (gate_up if k < BLOCKS else down)(i - 1, part * BLOCKS + k % BLOCKS)
                        if (part, k) in tasks:
                            tasks[part, k]()

            in_proj(0, misc_post(0, 0), 2)
            in_proj(0, misc_post(0, 1), 3)
            for u in range(4):
                add_unit(u)
            pre_turn(1, misc_pre(0, 0))
            in_proj(1, misc_pre(0, 1), 0)
            in_proj(1, misc_pre(0, 2), 1)
            for u in range(4, 8):
                add_unit(u)
            x_proj(1, misc_pre(0, 3))
            dt_proj(1, misc_pre(0, 4), 0)
            dt_proj(1, misc_pre(0, 5), 1)
            for u in range(8, UNITS):
                add_unit(u)
            out_proj(0, misc_post(0, 2))
            post_turn(0, misc_post(0, 3))
            pe.wait_ge(lo_done, NE)
            pe.wait_ge(wd_in, 16)
            body(1, tail=False)
            with pe.Fori(2, NC - 1) as i:
                body(i)
            body(NC - 1, pre=False)
            for part in range(PARTS):
                for k in range(BLOCKS):
                    gate_up(NC - 1, part * BLOCKS + k)
                    if (part, k) == (0, 1):
                        ffn_tail(NC - 2)
                if part == 0:
                    pe.wait_ge(wd_lo_done, 1)
                for k in range(BLOCKS):
                    down_split(part * BLOCKS + k)
            ffn_tail(NC - 1)

        @block.scalar
        def _(act):
            def turned(c, k, which, dst, s_done):
                act.wait_ge(misc_filled, k + 1)
                b = c // CB
                nc.scalar.activation(dst[:].rearrange("p (q t) -> p t q", t=TB),
                                     misc[:].rearrange("p (t q) -> p t q", t=TB), ACT.Identity,
                                     scale=mod_sb[:, b, which + 1:which + 2],
                                     bias=mod_sb[:, b, which:which + 1]).then_inc(s_done, 1)
                act.wait_ge(s_done, c + 1)
                act.sem_inc(misc_drained, 1)

            def pre_apply(c):
                act.wait_ge(ln_ready[0], c + 1)
                for t in range(TB):
                    last = nc.scalar.activation(tok[:, t, :], tok[:, t, :], ACT.Identity,
                                                scale=ln_rstd[:, 0, t:t + 1], bias=minus_mean[:, t:t + 1])
                last.then_inc(xn_ready[0], 1)

            def pre_h(c, k):
                turned(c, k, 0, h1, h1_ready)

            def post_h(c, k):
                if not is_first(c):
                    act.wait_ge(h2_ready, c)
                turned(c, k, 3, h2, h2_full)

            def take_xs(c, k, hf):
                act.wait_ge(misc_filled, k + 1)
                if not is_first(c):
                    act.wait_ge(conv_done, HALVES * c)
                src = second_bank(c, hf)
                nc.scalar.activation(xs_ext[:, hf, K - 1:], src[:], ACT.Copy).then_inc(xs_ready, 1)
                if hf == 0:
                    if not is_first(c):
                        act.wait_ge(du_ready, HALVES * c)
                    nc.scalar.activation(xc[:, hf, :], src[:], ACT.Identity, scale=cols[:, hf, K - 1:K],
                                         bias=cols[:, hf, K:K + 1]).then_inc(xs_ready, 1)
                act.wait_ge(xs_ready, 3 * c + hf + 2)
                act.sem_inc(misc_drained, 1)

            def silu_xc(c, hf):
                act.wait_ge(conv_done, HALVES * c + hf + 1)
                nc.scalar.activation(xc[:, hf, :], xc[:, hf, :], ACT.Silu).then_inc(xc_ready, 1)

            def take_xdbl(c, k):
                act.wait_ge(misc_filled, k + 1)
                if not is_first(c):
                    act.wait_ge(bc_stored, 16 * c)
                nc.scalar.activation(x_dbl[0:R + 2 * N, :], misc[0:R + 2 * N, :], ACT.Copy).then_inc(xdbl_ready, 1)
                act.wait_ge(xdbl_ready, c + 1)
                act.sem_inc(misc_drained, 1)

            def take_z(c, k, hf):
                act.wait_ge(misc_filled, k + 1)
                bias = cols[:, hf, K + 1:K + 2]
                nc.scalar.activation(tok_z[:, hf, :], second_bank(c, hf)[:], ACT.Identity, bias=bias)
                if not is_first(c):
                    act.wait_ge(delta_ready, HALVES * c)
                nc.scalar.activation(log_part[:, hf, :], second_bank(c, hf)[:], ACT.Abs, bias=bias).then_inc(z_ready, 1)
                act.wait_ge(z_ready, HALVES * c + hf + 1)
                act.sem_inc(misc_drained, 1)

            def softplus(c):
                act.wait_ge(z_ready, HALVES * (c + 1))
                for hf in range(HALVES):
                    nc.scalar.activation(log_part[:, hf, :], log_part[:, hf, :], ACT.Exp, scale=-1.0).then_inc(sp_step, 1)
                for hf in range(HALVES):
                    act.wait_ge(sp_step, HALVES * c + hf + 1)
                    nc.scalar.activation(log_part[:, hf, :], log_part[:, hf, :], ACT.Ln, bias=1.0).then_inc(sp_ready, 1)

            def exps(c, first, last_):
                for u in range(first, last_ + 1):
                    j, hf = u // HALVES, u % HALVES
                    act.wait_ge(delta_ready, HALVES * c + HALVES)
                    if is_first(c) and u < SLOTS:
                        act.wait_ge(lo_done, u + 1)
                    else:
                        act.wait_ge(unit_reduced, UNITS * c + u - SLOTS + 1)
                    for m in range(2):
                        n = 2 * j + m
                        last = nc.scalar.activation(ring[:, u % SLOTS, m, :], delta[:, hf, :], ACT.Exp,
                                                    scale=a_neg[:, hf, n:n + 1])
                    last.then_inc(exp_done, 1)

            def silu_gate(c, k, hf):
                act.wait_ge(misc_filled, k + 1)
                src = second_bank(c, hf) if is_first(c) else misc
                nc.scalar.activation(gate[:, hf, :], src[:], ACT.Silu).then_inc(gate_ready, 1)
                act.wait_ge(gate_ready, HALVES * c + hf + 1)
                act.sem_inc(misc_drained, 1)

            def silu_g(c, b):
                act.wait_ge(g_ready, NB * c + b + 1)
                nc.scalar.activation(p_tile[:, b % BLOCKS, :], g_bank[b % 2][:], ACT.Silu).then_inc(silu_done, 1)

            def split_p(b):
                act.wait_ge(p_ready, NB * (NC - 1) + b + 1)
                nc.scalar.activation(p_hi[:, b % BLOCKS, :], p_tile[:, b % BLOCKS, :], ACT.Copy).then_inc(p_hi_ready, 1)

            def ffn_out(c):
                act.wait_ge(acc_ready, c + 1)
                nc.scalar.activation(f_t, acc[:], ACT.Identity, scale=mod_sb[:, c // CB, 5:6]).then_inc(ft_ready, 1)

            act.wait_ge(mod_in, 16 * 2)
            nc.scalar.activation(sc[:], c_sb[:], ACT.Silu).then_inc(act_set, 1)
            pre_apply(0)
            act.wait_ge(dve_set, 6)
            pre_h(0, 0)
            act.wait_ge(small_in, 16 * 6)
            take_xs(0, 1, 0)
            take_xs(0, 2, 1)
            silu_xc(0, 0)
            silu_xc(0, 1)
            take_xdbl(0, 3)
            nc.scalar.preload_act_table_set(EXP_LN)
            nc.scalar.activation(a_neg[:], a_neg[:], ACT.Exp).then_inc(act_set, 1)
            act.wait_ge(act_set, 2)
            nc.scalar.activation(a_neg[:], a_neg[:], ACT.Copy, scale=-1.0).then_inc(act_set, 1)
            take_z(0, 4, 0)
            take_z(0, 5, 1)
            softplus(0)
            act.wait_ge(act_set, 3)
            exps(0, 0, 7)

            def body(i, pre=True, ffn=True):
                for part in range(PARTS):
                    if part in (1, 2) or (part == 3 and pre):
                        nc.scalar.preload_act_table_set(EXP_LN)
                    if part == 1:
                        exps(i, 8, 8)
                        if pre:
                            take_xs(i + 1, misc_pre(i, 2), 1)
                        exps(i, 9, 12)
                    if part == 2:
                        exps(i, 13, 13)
                        if pre:
                            take_z(i + 1, misc_pre(i, 5), 1)
                        exps(i, 14, 15)
                        if pre:
                            softplus(i + 1)
                    if part == 3 and pre:
                        exps(i + 1, 0, 3)
                    nc.scalar.preload_act_table(ACT.Silu)
                    behind = {}
                    if part == 0:
                        behind[-1] = lambda: silu_gate(i, misc_post(i, 0), 0)
                        behind[2] = lambda: silu_gate(i, misc_post(i, 1), 1)
                        if pre:
                            behind[3] = lambda: pre_apply(i + 1)
                            behind[5] = lambda: pre_h(i + 1, misc_pre(i, 0))
                            behind[7] = lambda: take_xs(i + 1, misc_pre(i, 1), 0)
                    if part == 1 and pre:
                        behind[0] = lambda: silu_xc(i + 1, 0)
                        behind[1] = lambda: silu_xc(i + 1, 1)
                        behind[3] = lambda: take_xdbl(i + 1, misc_pre(i, 3))
                        behind[5] = lambda: take_z(i + 1, misc_pre(i, 4), 0)
                    for k in range(-1, BLOCKS):
                        if ffn and k >= 0:
                            silu_g(i - 1, part * BLOCKS + k)
                        if k in behind:
                            behind[k]()
                if pre:
                    nc.scalar.preload_act_table_set(EXP_LN)
                    exps(i + 1, 4, 7)
                post_h(i, misc_post(i, 3))
                if ffn:
                    ffn_out(i - 1)

            body(0, ffn=False)
            with act.Fori(1, NC - 1) as i:
                body(i)
            body(NC - 1, pre=False)
            for part in range(PARTS):
                for b in range(part * BLOCKS, (part + 1) * BLOCKS):
                    silu_g(NC - 1, b)
                    if b > part * BLOCKS:
                        split_p(b - 1)
                split_p((part + 1) * BLOCKS - 1)
            ffn_out(NC - 1)

        @block.vector
        def _(dve):
            def norm_stats(which, c, src):
                step, base = ln_step[which], 4 * c
                stats, mv = ln_in[:, which], ln_mv[:, which]
                for t in range(TB):
                    last = nc.vector.bn_stats(stats[:, t, :], src(t))
                last.then_inc(step, 1)
                dve.wait_ge(step, base + 1)
                dve.sem_inc(step, 1)
                for t in range(TB):
                    last = nc.vector.bn_aggr(mv[:, t, :], stats[:, t, :])
                last.then_inc(step, 1)
                dve.wait_ge(step, base + 3)
                if which == 0:
                    nc.vector.tensor_scalar(minus_mean[:], mv[:, :, 0], -1.0, None, ALU.mult)
                nc.vector.tensor_scalar(ln_ve[:, which, :], mv[:, :, 1], EPS, None, ALU.add).then_inc(step, 1)

            def pre_stats(c):
                dve.wait_ge(x_loaded, 16 * (c + 1))
                norm_stats(0, c, lambda t: tok[:, t, :])

            def conv(c, hf):
                n_step, n_halo = ((K - 2) * HALVES + 1) * c + (K - 2) * hf, 2 * (HALVES * c + hf)
                nc.vector.tensor_copy(xs_ext[:, hf, 0:K - 1], halo[:, c % CB, hf, :]).then_inc(halo_in, 1)
                dve.wait_ge(halo_in, n_halo + 1)
                dve.wait_ge(xs_ready, 3 * c + hf + 2)
                nc.vector.tensor_copy(halo[:, c % CB + 1, hf, :], xs_ext[:, hf, L:]).then_inc(halo_in, 1)
                if hf == 1:
                    nc.vector.tensor_scalar(xc[:, hf, :], xs_ext[:, hf, K - 1:], cols[:, hf, K - 1:K],
                                            cols[:, hf, K:K + 1], ALU.mult, ALU.add).then_inc(conv_step, 1)
                for k in range(K - 1):
                    if k + hf > 0:
                        dve.wait_ge(conv_step, n_step + k + hf)
                    nc.vector.scalar_tensor_tensor(out=xc[:, hf, :], in0=xs_ext[:, hf, k:k + L],
                                                   scalar=cols[:, hf, k:k + 1], in1=xc[:, hf, :], op0=ALU.mult,
                                                   op1=ALU.add).then_inc(conv_step if k < K - 2 else conv_done, 1)
                dve.wait_ge(halo_in, n_halo + 2)
                dve.wait_ge(conv_done, HALVES * c + hf + 1)

            def finish_delta(c, hf):
                if hf == 0 and not is_first(c):
                    dve.wait_ge(exp_done, UNITS * c)
                dve.wait_ge(sp_ready, HALVES * c + hf + 1)
                nc.vector.scalar_tensor_tensor(out=delta[:, hf, :], in0=tok_z[:, hf, :], scalar=0.0,
                                               in1=log_part[:, hf, :], op0=ALU.max,
                                               op1=ALU.add).then_inc(delta_ready, 1)

            def take_du(c, hf):
                dve.wait_ge(delta_ready, HALVES * c + hf + 1)
                nc.vector.tensor_tensor(du[:, hf, :], delta[:, hf, :], xc[:, hf, :], ALU.mult).then_inc(du_ready, 1)

            def dbu(c, j, hf, m):
                if m == 0:
                    dve.wait_ge(b_loaded[j % 2], 16 * (PAIRS // 2 * c + j // 2 + 1))
                    dve.wait_ge(du_ready, HALVES * c + HALVES)
                if not (is_first(c) and j == 0 and hf == 0):
                    dve.wait_ge(scan_step, 2 * N * c + 2 * (HALVES * j + hf) + m - 1)
                nc.vector.tensor_tensor(dbu_bank[m][:], du[:, hf, :], b_tile[:, j % 2, m, :],
                                        ALU.mult).then_inc(dbu_done, 1)

            def scan(c, j, hf, m):
                u = HALVES * j + hf
                if m == 0:
                    dve.wait_ge(exp_done, UNITS * c + u + 1)
                dve.wait_ge(dbu_done, 2 * N * c + 2 * u + m + 1)
                n = 2 * j + m
                h = ring[:, u % SLOTS, m, :]
                nc.vector.tensor_tensor_scan(h, h, dbu_bank[m][:], carry[:, c % CB, hf, n:n + 1], ALU.mult,
                                             ALU.add).then_inc(scan_step, 1)

            def keep_carry(c, j, hf):
                u = HALVES * j + hf
                dve.wait_ge(scan_step, 2 * N * c + 2 * u + 2)
                nc.vector.tensor_copy(carry[:, c % CB + 1, hf, 2 * j:2 * j + 2],
                                      ring[:, u % SLOTS, :, L - 1]).then_inc(scan_done, 1)

            def times_c(c, u):
                j = u // HALVES
                dve.wait_ge(scan_done, UNITS * c + u + 1)
                dve.wait_ge(c_loaded[j % 4], 16 * (PAIRS // 4 * c + j // 4 + 1))
                hc = ring[:, u % SLOTS]
                nc.vector.tensor_tensor(hc, hc, c_tile[:, j % 4], ALU.mult).then_inc(hc_given, 1)

            def times_u(c, b):
                dve.wait_ge(silu_done, NB * c + b + 1)
                dve.wait_ge(u_ready, NB * c + b + 1)
                p = p_tile[:, b % BLOCKS, :]
                nc.vector.tensor_tensor(p, u_bank[b % 2][:], p, ALU.mult).then_inc(p_ready, 1)

            def gated(c, hf):
                if hf == 0:
                    dve.wait_ge(gate_ready, HALVES * (c + 1))
                    dve.wait_ge(unit_reduced, UNITS * (c + 1))
                y_hf = g_bank[hf][:] if is_first(c) else y[:, hf, :]
                nc.vector.tensor_tensor(gate[:, hf, :], gate[:, hf, :], y_hf, ALU.mult).then_inc(r_ready, 1)

            def residual(c, k):
                dve.wait_ge(misc_filled, k + 1)
                dve.wait_ge(xres_loaded, 16 * (c + 1))
                t = x1[:, c % 2].rearrange("p t h -> p (t h)")
                nc.vector.tensor_tensor(t, misc[:], t, ALU.add).then_inc(x1_ready, 1)
                dve.wait_ge(x1_ready, c + 1)
                dve.sem_inc(misc_drained, 1)

            def post_stats(c):
                norm_stats(1, c, lambda t: x1[:, c % 2, t, :])

            def post_apply(c):
                dve.wait_ge(ln_ready[1], c + 1)
                for t in range(TB):
                    last = nc.vector.tensor_scalar(tok2[:, t, :], x1[:, c % 2, t, :], ln_mv[:, 1, t, 0:1],
                                                   ln_rstd[:, 1, t:t + 1], ALU.subtract, ALU.mult)
                last.then_inc(xn_ready[1], 1)

            def split_h2(c):
                dve.wait_ge(h2_full, c + 1)
                nc.vector.tensor_copy(h2_hi[:], h2[:]).then_inc(h2_step, 1)
                dve.wait_ge(h2_step, c + 1)
                nc.vector.tensor_tensor(h2_lo[:], h2[:], h2_hi[:].bitcast(F32), ALU.subtract).then_inc(h2_ready, 1)

            def rest_of_p(b):
                dve.wait_ge(p_hi_ready, b + 1)
                p = p_tile[:, b % BLOCKS, :]
                nc.vector.tensor_tensor(p_lo[:, b % BLOCKS, :], p, p_hi[:, b % BLOCKS, :].bitcast(F32),
                                        ALU.subtract).then_inc(p_lo_ready, 1)

            def add_ffn(c):
                dve.wait_ge(ft_turned, c + 1)
                t = x1[:, c % 2].rearrange("p t h -> p (t h)")
                nc.vector.tensor_tensor(t, acc[:], t, ALU.add).then_inc(out_ready, 1)

            nc.vector.memset(halo[:], 0.0).then_inc(dve_set, 1)
            nc.vector.memset(carry[:], 0.0).then_inc(dve_set, 1)
            nc.vector.memset(sc_wide, 1.0).then_inc(dve_set, 1)
            pre_stats(0)
            dve.wait_ge(act_set, 1)
            dve.wait_ge(dve_set, 3)
            for b in range(B):
                last = nc.vector.tensor_scalar(sc_wide[:, b, :], sc_wide[:, b, :], sc[:, b:b + 1], None, ALU.mult)
            last.then_inc(dve_set, 1)
            dve.wait_ge(pe_set, 1)
            nc.vector.tensor_copy(mod_sb[:], acc[:, 0:6 * B].rearrange("p (k b) -> p b k", b=B)).then_inc(dve_set, 1)
            dve.wait_ge(dve_set, 5)
            for k in (1, 4):
                last = nc.vector.tensor_scalar(mod_sb[:, :, k], mod_sb[:, :, k], 1.0, None, ALU.add)
            last.then_inc(dve_set, 1)

            def clamp(v, sign, count):
                nc.vector.tensor_scalar(sign, v, 0.0, 2.0, ALU.is_ge, ALU.mult).then_inc(dve_set, 1)
                dve.wait_ge(dve_set, count + 1)
                nc.vector.tensor_scalar(sign, sign, -1.0, None, ALU.add).then_inc(dve_set, 1)
                dve.wait_ge(dve_set, count + 2)
                nc.vector.tensor_tensor(v, v, sign, ALU.mult).then_inc(dve_set, 1)
                dve.wait_ge(dve_set, count + 3)
                nc.vector.scalar_tensor_tensor(out=v, in0=v, scalar=0.25, in1=sign, op0=ALU.max,
                                               op1=ALU.mult).then_inc(dve_set, 1)
                dve.wait_ge(dve_set, count + 4)

            def take_hi(first, last_):
                for e in range(first, last_ + 1):
                    if e % 2 == 0:
                        dve.wait_ge(gu_in[e // 2], 16)
                    nc.vector.tensor_copy(gu_hi[:, e], ring[:, e]).then_inc(hi_done, 1)

            take_hi(0, 1)
            conv(0, 0)
            conv(0, 1)
            take_hi(2, 7)
            clamp(mod_sb[:, :, 5], gb_sign[:], 6)
            dve.wait_ge(pe_set, 2)
            nc.vector.tensor_copy(ga_row, u_bank[0][:, 0:B * H].rearrange("p (b h) -> p b h", b=B)).then_inc(dve_set, 1)
            dve.wait_ge(dve_set, 11)
            clamp(ga_row, ga_sign, 11)
            for b in range(B):
                for hf in range(HALVES):
                    last = nc.vector.tensor_tensor(w_out_ga[:, b, hf, :], w_out_sb[:, hf, :], ga_row[:, b, :], ALU.mult)
            last.then_inc(dve_set, 1)
            dve.wait_ge(dve_set, 16)
            for hf in range(HALVES):
                finish_delta(0, hf)
                take_du(0, hf)

            late = []

            def keep_late():
                if late:
                    keep_carry(*late.pop())

            def unit(c, u, *between):
                j, hf = u // HALVES, u % HALVES
                own = [lambda: dbu(c, j, hf, 0), lambda: dbu(c, j, hf, 1), lambda: scan(c, j, hf, 0),
                       lambda: scan(c, j, hf, 1)]
                for k, step in enumerate(own):
                    step()
                    if k == 0:
                        keep_late()
                    if k >= len(own) - len(between) and between[k - len(own) + len(between)]:
                        between[k - len(own) + len(between)]()
                late.append((c, j, hf))
                if between and between[-1]:
                    keep_late()

            for u in range(4):
                unit(0, u)
            keep_late()

            def body(i, pre=True, tail=True, done=0):
                blocks = iter(range(done, NB))

                def mults(n):
                    return [lambda b=next(blocks): times_u(i - 1, b) for _ in range(n)]

                def now(steps):
                    for step in steps:
                        step()

                if pre and not done:
                    pre_stats(i + 1)
                unit(i, 4, *mults(2 - min(done, 2)))
                if tail:
                    add_ffn(i - 2)
                m2, m3 = mults(2)
                unit(i, 5, m2, None, m3, None)
                unit(i, 6, *mults(4 - max(done - 2, 0)))
                keep_late()
                if pre:
                    conv(i + 1, 0)
                unit(i, 7)
                keep_late()
                if pre:
                    conv(i + 1, 1)
                    unit(i, 8, *mults(4))
                    unit(i, 9, *mults(2))
                    unit(i, 10, *mults(2))
                else:
                    unit(i, 8)
                    unit(i, 9, *mults(4))
                    unit(i, 10, *mults(4))
                unit(i, 11)
                unit(i, 12)
                if pre:
                    unit(i, 13, *mults(2))
                    unit(i, 14, *mults(4))
                    finish_delta(i + 1, 0)
                    finish_delta(i + 1, 1)
                    unit(i, 15, *mults(2))
                else:
                    unit(i, 13, *mults(4))
                    unit(i, 14, *mults(4))
                    unit(i, 15)
                    keep_late()
                times_c(i, HC_DVE)
                if pre:
                    take_du(i + 1, 0)
                    take_du(i + 1, 1)
                    dve.wait_ge(scan_done, UNITS * (i + 1))
                    m0, *m1_to_3 = mults(4)
                    unit(i + 1, 0, m0, None)
                    unit(i + 1, 1, *m1_to_3)
                else:
                    now(mults(4))
                for hf in range(HALVES):
                    gated(i, hf)
                    now(mults(1))
                if pre:
                    m6, m7 = mults(2)
                    unit(i + 1, 2, m6, None, m7, None)
                    keep_late()
                else:
                    now(mults(2))
                    dve.wait_ge(wd_in, 16)
                    nc.vector.tensor_copy(wd_hi[:], wd[:]).then_inc(wd_hi_done, 1)
                residual(i, misc_post(i, 2))
                post_stats(i)
                if pre:
                    unit(i + 1, 3, lambda: post_apply(i), None, None)
                    keep_late()
                else:
                    post_apply(i)
                split_h2(i)

            pre_stats(1)
            unit(0, 4)
            unit(0, 5)
            unit(0, 6)
            keep_late()
            conv(1, 0)
            unit(0, 7)
            keep_late()
            conv(1, 1)
            for u in range(8, UNITS):
                unit(0, u)
            keep_late()
            for hf in range(HALVES):
                finish_delta(1, hf)
                take_du(1, hf)
            dve.wait_ge(scan_done, UNITS)
            unit(1, 0)
            gated(0, 0)
            gated(0, 1)
            unit(1, 1)
            residual(0, misc_post(0, 2))
            post_stats(0)
            post_apply(0)
            split_h2(0)
            pre_stats(2)
            unit(1, 2, lambda: times_u(0, 0), lambda: times_u(0, 1))
            unit(1, 3, lambda: times_u(0, 2), lambda: times_u(0, 3))
            keep_late()
            body(1, tail=False, done=4)
            with dve.Fori(2, NC - 1) as i:
                body(i)
            body(NC - 1, pre=False)
            add_ffn(NC - 2)
            for part in range(PARTS):
                for b in range(part * BLOCKS, (part + 1) * BLOCKS):
                    times_u(NC - 1, b)
                    if b > part * BLOCKS:
                        rest_of_p(b - 1)
                rest_of_p((part + 1) * BLOCKS - 1)
            add_ffn(NC - 1)

        @block.gpsimd
        def _(pool):
            def rstd(which, c):
                pool.wait_ge(ln_step[which], 4 * (c + 1))
                nc.gpsimd.tensor_tensor(ln_rstd[:, which, :], ln_ve[:, which, :], minus_half[:],
                                        ALU.pow).then_inc(ln_ready[1] if which == 1 else ln1_rstd, 1)
                if which == 0:
                    pool.wait_ge(ln1_rstd, c + 1)
                    nc.gpsimd.tensor_tensor(minus_mean[:], minus_mean[:], ln_rstd[:, 0, :],
                                            ALU.mult).then_inc(ln_ready[0], 1)

            def times_c(c, u):
                j, hf = u // HALVES, u % HALVES
                if u == HC_DVE and not is_first(c):
                    pool.wait_ge(hc_given, c)
                    pool.sem_inc(pool_step, 1)
                    return
                pool.wait_ge(scan_done, UNITS * c + u + 1)
                if hf == 0:
                    pool.wait_ge(c_loaded[j % 4], 16 * (PAIRS // 4 * c + j // 4 + 1))
                hc = ring[:, u % SLOTS]
                nc.gpsimd.tensor_tensor(hc, hc, c_tile[:, j % 4],
                                        ALU.mult).then_inc(hc_ready if is_first(c) else pool_step, 1)

            def add_up(c, u):
                j, hf = u // HALVES, u % HALVES
                hc = ring[:, u % SLOTS]
                step = 2 * (UNITS * (c - 1) + u)
                pool.wait_ge(pool_step, step + 1)
                nc.gpsimd.tensor_tensor(hc[:, 0, :], hc[:, 0, :], hc[:, 1, :], ALU.add).then_inc(pool_step, 1)
                if j == 0:
                    return
                pool.wait_ge(pool_step, step + 2)
                if j == 1:
                    if hf == 0:
                        pool.wait_ge(r_ready, HALVES * c)
                    so_far = ring[:, (u - HALVES) % SLOTS, 0, :]
                else:
                    pool.wait_ge(unit_reduced, UNITS * c + u - 1)
                    so_far = y[:, hf, :]
                nc.gpsimd.tensor_tensor(y[:, hf, :], so_far, hc[:, 0, :], ALU.add).then_inc(unit_reduced, 1)
                if (j, hf) == (1, 1):
                    pool.wait_ge(unit_reduced, UNITS * c + 2)
                    pool.sem_inc(unit_reduced, 2)

            def reduce_unit(c, u):
                times_c(c, u)
                add_up(c, u)

            nc.gpsimd.memset(minus_half[:], -0.5).then_inc(pool_set, 1)
            nc.gpsimd.memset(ident[:], 0.0).then_inc(pool_set, 1)
            pool.wait_ge(pool_set, 2)
            nc.gpsimd.affine_select(out=ident[:], in_=ident[:], compare_op=ALU.not_equal, fill=1.0, base=0,
                                    pattern=[[-1, P]], channel_multiplier=1).then_inc(pool_set, 1)
            rstd(0, 0)
            for e in range(NE):
                pool.wait_ge(hi_done, e + 1)
                nc.gpsimd.tensor_tensor(gu_lo[:, e], ring[:, e], gu_hi[:, e].bitcast(F32),
                                        ALU.subtract).then_inc(lo_done, 1)
            for u in range(4):
                times_c(0, u)

            def body(i, pre=True, ln_done=False):
                if not ln_done:
                    reduce_unit(i, 3)
                    if pre:
                        rstd(0, i + 1)
                for u in range(4, UNITS):
                    reduce_unit(i, u)
                if pre:
                    reduce_unit(i + 1, 0)
                    reduce_unit(i + 1, 1)
                    times_c(i + 1, 2)
                rstd(1, i)
                if pre:
                    add_up(i + 1, 2)

            rstd(0, 1)
            for u in range(4, UNITS):
                times_c(0, u)
            reduce_unit(1, 0)
            rstd(1, 0)
            rstd(0, 2)
            for u in range(1, 4):
                reduce_unit(1, u)
            body(1, ln_done=True)
            with pool.Fori(2, NC - 1) as i:
                body(i)
            body(NC - 1, pre=False)
            pool.wait_ge(wd_hi_done, 1)
            nc.gpsimd.tensor_tensor(wd_lo[:], wd[:], wd_hi[:].bitcast(F32), ALU.subtract).then_inc(wd_lo_done, 1)


def kernel(**inputs):
    import numpy as np
    import concourse.bacc as bacc
    from concourse.bass_utils import run_bass_kernel_spmd

    a = {k: np.asarray(v) for k, v in inputs.items()}

    def halves(t):
        return t.reshape(HALVES, P, -1).transpose(1, 0, 2)

    cols = np.concatenate([halves(a["L0_attn_conv_w"].reshape(D, K)), halves(a["L0_attn_conv_b"].reshape(D, 1)),
                           halves(a["L0_attn_b_dt"].reshape(D, 1))], axis=2)
    gu = np.stack([a["L0_ffn_Wg"], a["L0_ffn_Wu"]], axis=2)
    arrays = {
        "x": a["L0_attn_x"].reshape(NC * P, TB * H),
        "w_in": a["L0_attn_W_in"].T,
        "cols": cols,
        "w_x": halves(a["L0_attn_W_x"].T),
        "w_dt": a["L0_attn_W_dt"].T,
        "a_log": halves(a["L0_attn_A_log"]),
        "w_out": halves(a["L0_attn_W_out"].T),
        "w_gu": gu.transpose(1, 0, 2, 3),
        "w_d": a["L0_ffn_Wd"].reshape(NB, P, H).transpose(1, 0, 2),
        "c_t": a["L0_c"].T,
        "w_mod": a["L0_wmod"],
    }
    arrays = {k: np.ascontiguousarray(v) for k, v in arrays.items()}
    nc = bacc.Bacc("TRN2", target_bir_lowering=False, num_devices=1)
    t = {k: nc.dram_tensor("in_" + k, v.shape, F32, kind="ExternalInput").ap() for k, v in arrays.items()}
    out = nc.dram_tensor("out_tokens", (NC * P, TB * H), F32, kind="ExternalOutput").ap()
    bc_dram = nc.dram_tensor("bc_rows", (NC * 2 * N, L), F32, kind="Internal").ap()
    build(nc, t["x"], t["w_in"], t["cols"], t["w_x"], t["w_dt"], t["a_log"], t["w_out"], t["w_gu"],
          t["w_d"], t["c_t"], t["w_mod"], out, bc_dram)
    r = run_bass_kernel_spmd(nc, [{"in_" + k: v for k, v in arrays.items()}], core_ids=[0])
    return r.results[0]["out_tokens"].reshape(B, S, H)
```
